# Optimizing a Trainium2 kernel written in Bass

```python
import numpy as np
import jax
import jax.numpy as jnp

def _softmax(x, axis=-1):
    return jax.nn.softmax(x, axis=axis)

def _gelu(x):
    return jax.nn.gelu(x, approximate=True)

def _silu(x):
    return jax.nn.silu(x)

def _sigmoid(x):
    return jax.nn.sigmoid(x)

def _layernorm(x, axis=-1, eps=1e-05):
    m = jnp.mean(x, axis=axis, keepdims=True)
    v = jnp.var(x, axis=axis, keepdims=True)
    return (x - m) / jnp.sqrt(v + eps)

def _scatter_add(tgt, idx, src, axis=0):
    return tgt.at[idx].add(src)

def _segment_sum(src, seg, n):
    return jax.ops.segment_sum(src, seg, n)
kernel_name = 'mk_vit_tower_d1_tok_img1024_r4_8afc2c'

def setup_inputs(seed: int=0):
    np.random.seed(seed)
    _w = jnp.asarray

    def _rec_inputs():
        import jax
        import jax.numpy as jnp
        _rk = jax.random.key(seed)
        x = -0.00016672 + 0.999947 * jax.random.normal(jax.random.fold_in(_rk, 1), (64, 3, 96, 96), jnp.float32)
        return x
    x = _rec_inputs()

    def _L0_tok_setup():
        import jax, jax.numpy as jnp
        import numpy as np
        EPS = 1e-05

        def _layernorm(x, w, b):
            mu = jnp.mean(x, axis=-1, keepdims=True)
            var = jnp.mean(jnp.square(x - mu), axis=-1, keepdims=True)
            return (x - mu) * jax.lax.rsqrt(var + EPS) * w + b
        key = jax.random.key(seed)
        ks = jax.random.split(key, 8)
        B, C, H, W = (64, 3, 96, 96)
        P, D = (16, 256)
        patch_dim = C * P * P
        num_patches = H // P * (W // P)
        x = jax.random.normal(ks[0], (B, C, H, W), dtype=jnp.float32)
        ln1_w = jnp.ones((patch_dim,), jnp.float32)
        ln1_b = jnp.zeros((patch_dim,), jnp.float32)
        lin_w = jax.random.normal(ks[1], (patch_dim, D), jnp.float32) / np.sqrt(patch_dim)
        lin_b = jnp.zeros((D,), jnp.float32)
        ln2_w = jnp.ones((D,), jnp.float32)
        ln2_b = jnp.zeros((D,), jnp.float32)
        pos_embedding = jax.random.normal(ks[2], (1, num_patches + 1, D), jnp.float32)
        cls_token = jax.random.normal(ks[3], (1, 1, D), jnp.float32)
        return dict(x=x, ln1_w=ln1_w, ln1_b=ln1_b, lin_w=lin_w, lin_b=lin_b, ln2_w=ln2_w, ln2_b=ln2_b, pos_embedding=pos_embedding, cls_token=cls_token)
    _L0_tok_all = _L0_tok_setup()
    _L0_tok_in = {k: v for k, v in _L0_tok_all.items() if k in ('ln1_w', 'ln1_b', 'lin_w', 'lin_b', 'ln2_w', 'ln2_b', 'pos_embedding', 'cls_token')}
    del _L0_tok_all

    def _L0_attn_setup():
        import jax, jax.numpy as jnp
        import numpy as np
        import math
        D_MODEL = 256
        NUM_HEADS = 16
        D_K = D_MODEL // NUM_HEADS
        B, S = (2, 512)

        def _linear_weight(key, out_f, in_f):
            return jax.random.normal(key, (out_f, in_f), jnp.float32) * math.sqrt(2.0 / in_f)
        key = jax.random.key(seed)
        ks = jax.random.split(key, 5)
        x = jax.random.normal(ks[0], (B, S, D_MODEL), jnp.float32)
        return {'x': x, 'Wq': _linear_weight(ks[1], D_MODEL, D_MODEL), 'bq': jnp.zeros((D_MODEL,), jnp.float32), 'Wk': _linear_weight(ks[2], D_MODEL, D_MODEL), 'bk': jnp.zeros((D_MODEL,), jnp.float32), 'Wv': _linear_weight(ks[3], D_MODEL, D_MODEL), 'bv': jnp.zeros((D_MODEL,), jnp.float32), 'Wo': _linear_weight(ks[4], D_MODEL, D_MODEL), 'bo': jnp.zeros((D_MODEL,), jnp.float32)}
    _L0_attn_all = _L0_attn_setup()
    _L0_attn_in = {k: v for k, v in _L0_attn_all.items() if k in ('Wq', 'bq', 'Wk', 'bk', 'Wv', 'bv', 'Wo', 'bo')}
    del _L0_attn_all

    def _L0_ffn_setup():
        import jax, jax.numpy as jnp
        import numpy as np
        B, T, D = (2, 512, 256)
        DCD = 1024
        RET = 128
        NEXP = 1024
        NKEYS = 64
        H = 4
        KPH = 8
        key = jax.random.key(seed)
        ks = jax.random.split(key, 10)
        s = lambda k, shape, scale: jax.random.normal(k, shape, jnp.float32) * scale
        return {'hidden_states': jax.random.normal(ks[0], (B, T, D), jnp.float32), 'Wg': s(ks[1], (D, DCD), 0.02), 'bg': jnp.zeros((DCD,), jnp.float32), 'Wu': s(ks[2], (D, DCD), 0.02), 'bu': jnp.zeros((DCD,), jnp.float32), 'Wd': s(ks[3], (DCD, D), 0.02), 'bd': jnp.zeros((D,), jnp.float32), 'Wq': s(ks[4], (D, RET * H), 0.02), 'keys': s(ks[5], (H, NKEYS, 2, RET // 2), 0.02), 'down_embed': s(ks[6], (NEXP, D), 0.02), 'up_embed': s(ks[7], (NEXP, D), 0.02)}
    _L0_ffn_all = _L0_ffn_setup()
    _L0_ffn_in = {k: v for k, v in _L0_ffn_all.items() if k in ('Wg', 'bg', 'Wu', 'bu', 'Wd', 'bd', 'Wq', 'keys', 'down_embed', 'up_embed')}
    del _L0_ffn_all
    return {'x': x, 'L0_tok_ln1_w': _L0_tok_in['ln1_w'], 'L0_tok_ln1_b': _L0_tok_in['ln1_b'], 'L0_tok_lin_w': _L0_tok_in['lin_w'], 'L0_tok_lin_b': _L0_tok_in['lin_b'], 'L0_tok_ln2_w': _L0_tok_in['ln2_w'], 'L0_tok_ln2_b': _L0_tok_in['ln2_b'], 'L0_tok_pos_embedding': _L0_tok_in['pos_embedding'], 'L0_tok_cls_token': _L0_tok_in['cls_token'], 'L0_attn_Wq': _L0_attn_in['Wq'], 'L0_attn_bq': _L0_attn_in['bq'], 'L0_attn_Wk': _L0_attn_in['Wk'], 'L0_attn_bk': _L0_attn_in['bk'], 'L0_attn_Wv': _L0_attn_in['Wv'], 'L0_attn_bv': _L0_attn_in['bv'], 'L0_attn_Wo': _L0_attn_in['Wo'], 'L0_attn_bo': _L0_attn_in['bo'], 'L0_ffn_Wg': _L0_ffn_in['Wg'], 'L0_ffn_bg': _L0_ffn_in['bg'], 'L0_ffn_Wu': _L0_ffn_in['Wu'], 'L0_ffn_bu': _L0_ffn_in['bu'], 'L0_ffn_Wd': _L0_ffn_in['Wd'], 'L0_ffn_bd': _L0_ffn_in['bd'], 'L0_ffn_Wq': _L0_ffn_in['Wq'], 'L0_ffn_keys': _L0_ffn_in['keys'], 'L0_ffn_down_embed': _L0_ffn_in['down_embed'], 'L0_ffn_up_embed': _L0_ffn_in['up_embed']}

def reference(x, L0_tok_ln1_w, L0_tok_ln1_b, L0_tok_lin_w, L0_tok_lin_b, L0_tok_ln2_w, L0_tok_ln2_b, L0_tok_pos_embedding, L0_tok_cls_token, L0_attn_Wq, L0_attn_bq, L0_attn_Wk, L0_attn_bk, L0_attn_Wv, L0_attn_bv, L0_attn_Wo, L0_attn_bo, L0_ffn_Wg, L0_ffn_bg, L0_ffn_Wu, L0_ffn_bu, L0_ffn_Wd, L0_ffn_bd, L0_ffn_Wq, L0_ffn_keys, L0_ffn_down_embed, L0_ffn_up_embed):
    import jax
    import jax.numpy as jnp

    def _L0_tok_ref(x, ln1_w, ln1_b, lin_w, lin_b, ln2_w, ln2_b, pos_embedding, cls_token):
        import jax, jax.numpy as jnp
        import numpy as np
        EPS = 1e-05

        def _layernorm(x, w, b):
            mu = jnp.mean(x, axis=-1, keepdims=True)
            var = jnp.mean(jnp.square(x - mu), axis=-1, keepdims=True)
            return (x - mu) * jax.lax.rsqrt(var + EPS) * w + b
        B, C, H, W = x.shape
        P = 16
        h, w = (H // P, W // P)
        patches = x.reshape(B, C, h, P, w, P)
        patches = patches.transpose(0, 2, 4, 3, 5, 1)
        patches = patches.reshape(B, h * w, P * P * C)
        y = _layernorm(patches, ln1_w, ln1_b)
        y = jnp.einsum('bnp,pd->bnd', y, lin_w) + lin_b
        y = _layernorm(y, ln2_w, ln2_b)
        cls = jnp.broadcast_to(cls_token, (B, 1, y.shape[-1]))
        y = jnp.concatenate([cls, y], axis=1)
        n = h * w
        y = y + pos_embedding[:, :n + 1]
        return y

    def _L0_attn_ref(x, Wq, bq, Wk, bk, Wv, bv, Wo, bo):
        import jax, jax.numpy as jnp
        import numpy as np
        import math
        D_MODEL = 256
        NUM_HEADS = 16
        D_K = D_MODEL // NUM_HEADS
        B, S = (2, 512)

        def _linear_weight(key, out_f, in_f):
            return jax.random.normal(key, (out_f, in_f), jnp.float32) * math.sqrt(2.0 / in_f)
        b, s, _ = x.shape
        q = jnp.einsum('bsd,ed->bse', x, Wq) + bq
        k = jnp.einsum('bsd,ed->bse', x, Wk) + bk
        v = jnp.einsum('bsd,ed->bse', x, Wv) + bv
        q = q.reshape(b, s, NUM_HEADS, D_K).transpose(0, 2, 1, 3)
        k = k.reshape(b, s, NUM_HEADS, D_K).transpose(0, 2, 1, 3)
        v = v.reshape(b, s, NUM_HEADS, D_K).transpose(0, 2, 1, 3)
        scores = jnp.einsum('bhqd,bhkd->bhqk', q, k) / math.sqrt(D_K)
        attn = jax.nn.softmax(scores, axis=-1)
        out = jnp.einsum('bhqk,bhkd->bhqd', attn, v)
        out = out.transpose(0, 2, 1, 3).reshape(b, s, D_MODEL)
        return jnp.einsum('bsd,ed->bse', out, Wo) + bo

    def _L0_ffn_ref(hidden_states, Wg, bg, Wu, bu, Wd, bd, Wq, keys, down_embed, up_embed):
        import jax, jax.numpy as jnp
        import numpy as np
        B, T, D = (2, 512, 256)
        DCD = 1024
        RET = 128
        NEXP = 1024
        NKEYS = 64
        H = 4
        KPH = 8
        b, t, d = hidden_states.shape
        q = (hidden_states @ Wq).reshape(b, t, 2, H, RET // 2)
        sim = jnp.einsum('btphn,hkpn->pbthk', q, keys)
        sc, ix = jax.lax.top_k(sim, KPH)
        sx, sy = (sc[0], sc[1])
        ixx, ixy = (ix[0], ix[1])
        all_sc = (sx[..., :, None] + sy[..., None, :]).reshape(b, t, H, KPH * KPH)
        all_ix = (ixx[..., :, None] * NKEYS + ixy[..., None, :]).reshape(b, t, H, KPH * KPH)
        scores, pk = jax.lax.top_k(all_sc, KPH)
        idx = jnp.take_along_axis(all_ix, pk, axis=-1)
        de = down_embed[idx]
        ue = up_embed[idx]
        w = jnp.einsum('btd,bthkd->bthk', hidden_states, de)
        w = jax.nn.silu(w) * jax.nn.softmax(scores, axis=-1)
        experts_states = jnp.einsum('bthk,bthkd->btd', w, ue)
        mlp = jax.nn.silu(hidden_states @ Wg + bg) * (hidden_states @ Wu + bu) @ Wd + bd
        return mlp + experts_states
    h = _L0_tok_ref(x, L0_tok_ln1_w, L0_tok_ln1_b, L0_tok_lin_w, L0_tok_lin_b, L0_tok_ln2_w, L0_tok_ln2_b, L0_tok_pos_embedding, L0_tok_cls_token)
    h = h + _L0_attn_ref(_layernorm(h, axis=-1), L0_attn_Wq, L0_attn_bq, L0_attn_Wk, L0_attn_bk, L0_attn_Wv, L0_attn_bv, L0_attn_Wo, L0_attn_bo)
    h = h + _L0_ffn_ref(_layernorm(h, axis=-1), L0_ffn_Wg, L0_ffn_bg, L0_ffn_Wu, L0_ffn_bu, L0_ffn_Wd, L0_ffn_bd, L0_ffn_Wq, L0_ffn_keys, L0_ffn_down_embed, L0_ffn_up_embed)
    return h

_drawn_inputs = setup_inputs


def setup_inputs(seed=0):
    import zlib

    import numpy as np

    out = dict(_drawn_inputs(seed))
    spreads = {'L0_tok_ln1_w': (1.0, 0.2),
     'L0_tok_ln1_b': (0.0, 0.1),
     'L0_tok_lin_b': (0.0, 0.1),
     'L0_tok_ln2_w': (1.0, 0.2),
     'L0_tok_ln2_b': (0.0, 0.1),
     'L0_attn_bq': (0.0, 0.1),
     'L0_attn_bk': (0.0, 0.8),
     'L0_attn_bv': (0.0, 0.1),
     'L0_attn_bo': (0.0, 0.1),
     'L0_ffn_bg': (0.0, 0.8),
     'L0_ffn_bu': (0.0, 0.8),
     'L0_ffn_bd': (0.0, 0.1)}
    factors = {'L0_ffn_Wg': 2.978,
     'L0_ffn_Wu': 2.962,
     'L0_ffn_Wd': 2.819,
     'L0_ffn_Wq': 8.0,
     'L0_ffn_keys': 8.0,
     'L0_ffn_down_embed': 8.0,
     'L0_ffn_up_embed': 8.0}
    for name, (base, spread) in spreads.items():
        noise = np.random.default_rng([zlib.crc32(name.encode()), seed]).standard_normal(out[name].shape)
        drawn = base * np.exp(spread * noise) if base else spread * noise
        out[name] = jnp.asarray(drawn.astype(out[name].dtype))
    for name, factor in factors.items():
        out[name] = (out[name] * factor).astype(out[name].dtype)
    return out
```

```python
from contextlib import ExitStack

import concourse.bass as bass
from concourse import mybir

F32 = mybir.dt.float32
BF16 = mybir.dt.bfloat16
ALU = mybir.AluOpType
ACT = mybir.ActivationFunctionType
AX = mybir.AxisListType.X

B, CH, IMG, P = 64, 3, 96, 16
NP_ = (IMG // P) ** 2
S = NP_ + 1
PD = P * P * CH
D = 256
H, DK = 16, 16
G = 3
R = G * S
C = R + 1
NA = -(-B // G)
KP = PD // 128
KD = D // 128
HC = H // KD
HB = H // 4
N = B * S
NB = -(-N // 128)
F = 1024
KF = F // 128
PH, NK, RET = 4, 64, 64
NE = 1024
XR = NE // NK
T8 = 8
EPS = 1e-5
BIG = 65536.0


def late(t, n):
    return not isinstance(t, int) or t >= n


def steps(engine, body, n, ahead, behind):
    first = -ahead
    lo = 4
    hi = n - ahead
    hi -= (hi - lo) % 2
    for t in range(first, lo):
        body(t // 2, t % 2, lambda k, t=t: 0 <= t + k < n)
    with engine.Fori(lo // 2, hi // 2) as j:
        for u in (0, 1):
            body(j, u, lambda k: True)
    for t in range(hi, n + behind):
        body(t // 2, t % 2, lambda k, t=t: 0 <= t + k < n)


def tile_at(j, u, k):
    q = u + k
    return 2 * j + q, j + q // 2, q % 2


def vit_tower(nc, I, out, h1_dram):
    with ExitStack() as ctx:
        def sb(name, shape, dt=F32):
            return ctx.enter_context(nc.sbuf_tensor(name, shape, dt))

        def sem(name):
            return ctx.enter_context(nc.semaphore(name))

        ident = sb("ident", [128, 128])
        nident = sb("nident", [C, C])
        headmask = sb("headmask", [128, HC])
        lin_w = sb("lin_w", [128, KP, D])
        ln1_w = sb("ln1_w", [128, KP])
        ln1_b = sb("ln1_b", [128, KP])
        ln1_b_rep = sb("ln1_b_rep", [128, KP, C])
        lin_bias = sb("lin_bias", [C, D])
        ln2_w = sb("ln2_w", [C, D])
        pos = sb("pos", [C, D])
        pos_add = sb("pos_add", [C, D])
        wq = sb("wq", [128, KD, D])
        wk = sb("wk", [128, KD, D])
        wv = sb("wv", [128, KD, D])
        wo = sb("wo", [128, KD, D])
        bq = sb("bq", [128, KD])
        bk = sb("bk", [128, KD])
        bv = sb("bv", [C, D])
        bo = sb("bo", [C, D])
        mask_f = sb("mask_f", [4, 2 * C + 2 * HB * C])
        mask_b = sb("mask_b", [4, 2 * C + 2 * HB * C], BF16)
        sum_lhs = sb("sum_lhs", [C + 4, C], BF16)
        eps = sb("eps", [128, 1])
        mhalf = sb("mhalf", [128, 1])
        wg = sb("wg", [128, KD, F])
        wu = sb("wu", [128, KD, F])
        wd = sb("wd", [128, KF, D])
        bg = sb("bg", [128, KF])
        bg_half = sb("bg_half", [128, KF])
        bu = sb("bu", [128, KF])
        bd = sb("bd", [128, D])
        wqf = sb("wqf", [RET, 2 * PH, D])
        keys = sb("keys", [RET, 2 * PH, NK])
        simw = sb("simw", [128, KD, 2 * PH * NK])
        down = sb("down", [128, KD, NE])
        up = sb("up", [128, NE // 128, D])

        w_a = sem("w_a")
        w_b = sem("w_b")
        w_b2 = sem("w_b2")
        const_f = sem("const_f")
        const_c = sem("const_c")
        mask_ready = sem("mask_ready")
        mask_moved = sem("mask_moved")
        rep_ready = sem("rep_ready")
        fold_ready = sem("fold_ready")
        bias_ps = sem("bias_ps")
        pos_ready = sem("pos_ready")
        pos_zero = sem("pos_zero")
        phase_a_ready = sem("phase_a_ready")
        h1_stored = [sem("h1_stored0"), sem("h1_stored1")]

        with ExitStack() as ca:
            def sa(name, shape, dt=F32):
                return ca.enter_context(nc.sbuf_tensor(name, shape, dt))

            def pa(name, shape):
                return ca.enter_context(nc.psum_tensor(name, shape, F32))

            xin = sa("xin", [C, 2, PD])
            xn = sa("xn", [C, 2, PD])
            st1 = sa("st1", [C, 2, 12])
            st2 = sa("st2", [C, 2, 6])
            st3 = sa("st3", [C, 2, 6])
            mv1 = sa("mv1", [C, 2, 2])
            mv2 = sa("mv2", [C, 2, 2])
            mv3 = sa("mv3", [C, 2, 2])
            ve = sa("ve", [C, 3, 1])
            rstd = sa("rstd", [C, 3, 2])
            xT = sa("xT", [128, KP, C])
            y = sa("y", [C, D])
            yn = sa("yn", [C, D])
            yw = sa("yw", [C, D])
            h = sa("h", [C, 2, D])
            hb = sa("hb", [C, 2, D])
            hn = sa("hn", [C, D])
            hnT = sa("hnT", [128, KD, C])
            qT = sa("qT", [128, KD, C])
            kT = sa("kT", [128, KD, C])
            qTb = sa("qTb", [128, KD, C], BF16)
            q_exp = sa("q_exp", [128, KD, HC, C])
            k_exp = sa("k_exp", [128, KD, HC, C], BF16)
            v_aug = sa("v_aug", [C, 2, H, DK + 1])
            mx = sa("mx", [C, H])
            diag = sa("diag", [C + 4, H, C], BF16)
            pT = sa("pT", [C, H, C])
            rden = sa("rden", [C, H])
            o = sa("o", [C, D])
            oT = sa("oT", [128, KD, C])
            h1 = sa("h1", [C, 2, D])

            ps_x = pa("ps_x", [128, 512])
            ps_y = pa("ps_y", [128, 512])
            ps_l = pa("ps_l", [128, 512])
            ps_o = pa("ps_o", [128, 512])
            ps_s = pa("ps_s", [128, 4, 512])

            x_loaded = [ctx.enter_context(nc.semaphore(f"x_loaded{u}")) for u in (0, 1)]
            st1_ready = sem("st1_ready")
            mv1_ready = sem("mv1_ready")
            st2_ready = sem("st2_ready")
            mv2_ready = sem("mv2_ready")
            st3_ready = sem("st3_ready")
            mv3_ready = sem("mv3_ready")
            ve_ready = [ctx.enter_context(nc.semaphore(f"ve_ready{k}")) for k in range(3)]
            rstd1_ready = sem("rstd1_ready")
            rstd2_ready = sem("rstd2_ready")
            rstd3_ready = sem("rstd3_ready")
            xn_ready = sem("xn_ready")
            xT_ps = sem("xT_ps")
            xT_ready = sem("xT_ready")
            lin_ps = sem("lin_ps")
            y_ready = sem("y_ready")
            yn_ready = sem("yn_ready")
            yw_ready = sem("yw_ready")
            h_ready = sem("h_ready")
            hb_ready = sem("hb_ready")
            hn_ready = sem("hn_ready")
            hnT_ps = sem("hnT_ps")
            hnT_ready = sem("hnT_ready")
            qk_ps = sem("qk_ps")
            v_ps = sem("v_ps")
            qk_ready = sem("qk_ready")
            qb_ready = sem("qb_ready")
            kexp_ready = sem("kexp_ready")
            qexp_ready = sem("qexp_ready")
            v_ready = sem("v_ready")
            s_ps = sem("s_ps")
            max_ready = sem("max_ready")
            diag_ready = sem("diag_ready")
            st_ps = sem("st_ps")
            p_ready = sem("p_ready")
            pv_ps = sem("pv_ps")
            rden_ready = sem("rden_ready")
            o_ready = sem("o_ready")
            oT_ps = sem("oT_ps")
            oT_ready = sem("oT_ready")
            wo_ps = sem("wo_ps")
            h1_ready = sem("h1_ready")

            block = ca.enter_context(nc.Block())

            loads_a = [
                (ident[:, :], I["ident"]), (headmask[:, :], I["headmask"]),
                (nident[:, :], I["nident"]), (mask_f[:, :], I["mask"]),
                (ln1_w[:, :], I["ln1_w"]), (ln1_b[:, :], I["ln1_b"]),
                (lin_w[:, :, :], I["lin_w"]),
                (lin_bias[:, :], I["lin_b"].to_broadcast([C, D])),
                (wq[:, :, :], I["wq"]), (wk[:, :, :], I["wk"]), (wv[:, :, :], I["wv"]),
                (wo[:, :, :], I["wo"]), (bq[:, :], I["bq"]), (bk[:, :], I["bk"]),
                (bv[:, :], I["bv"].to_broadcast([C, D])), (bo[:, :], I["bo"].to_broadcast([C, D])),
            ]
            loads_rows = []
            for g in range(G):
                loads_rows += [
                    (ln2_w[g * S + 1:(g + 1) * S, :], I["ln2_w"].to_broadcast([NP_, D])),
                    (pos_add[g * S + 1:(g + 1) * S, :], I["ln2_b"].to_broadcast([NP_, D])),
                    (pos_add[g * S:g * S + 1, :], I["cls"]),
                    (pos[g * S:(g + 1) * S, :], I["pos"]),
                ]
            loads_b = [
                (wqf[:, :, :], I["wqf"]), (keys[:, :, :], I["keys"]), (down[:, :, :], I["down"]),
                (wg[:, :, :], I["wg"]), (wu[:, :, :], I["wu"]), (bg[:, :], I["bg"]), (bu[:, :], I["bu"]),
                (wd[:, :, :], I["wd"]), (up[:, :, :], I["up"]), (bd[:, :], I["bd"].to_broadcast([128, D])),
            ]
            n_loads_a = 16 * len(loads_a)
            n_loads_rows = 16 * len(loads_rows)

            @block.sync
            def _(sp):
                def load_x(t, j, u):
                    if late(t, 2):
                        sp.wait_ge(xn_ready, t - 1)
                    sp.dma_start(xin[:, u, :], I["x"][t, :, :]).then_inc(x_loaded[u], 16)

                def store(t, j, u):
                    sp.wait_ge(h1_ready, t + 1)
                    if isinstance(t, int) and t == NA - 1:
                        new = B - (NA - 1) * G
                        sp.dma_start(h1_dram[(B - new) * S:B * S, :],
                                     h1[R - new * S:R, u, :]).then_inc(h1_stored[u], 16)
                    else:
                        sp.dma_start(h1_dram[bass.ds(t * R, R), :], h1[0:R, u, :]).then_inc(h1_stored[u], 16)

                def body(j, u, has):
                    if has(4):
                        load_x(*tile_at(j, u, 4))
                    if has(-1):
                        store(*tile_at(j, u, -1))

                for dst, src in loads_a:
                    sp.dma_start(dst, src).then_inc(w_a, 16)
                sp.wait_ge(pos_zero, 3)
                for dst, src in loads_rows:
                    sp.dma_start(dst, src).then_inc(w_b, 16)
                sp.wait_ge(mask_ready, 1)
                for r in range(H // HB):
                    sp.dma_start(diag[C:C + 4, r * HB:(r + 1) * HB, :],
                                 mask_b[:, 2 * C + HB * C:2 * C + 2 * HB * C]
                                 .rearrange("p (a b) -> p a b", a=HB)).then_inc(mask_moved, 16)
                sp.wait_ge(const_c, 1)
                sp.dma_start(sum_lhs[C:C + 4, :], mask_b[:, C:2 * C]).then_inc(mask_moved, 16)
                steps(sp, body, NA, 4, 1)
                for u in (0, 1):
                    sp.wait_ge(h1_stored[u], 16 * ((NA + 1 - u) // 2))

            @block.gpsimd
            def _(pool):
                pool.memset(ln2_w[:, :], 0.0).then_inc(pos_zero, 1)
                pool.memset(pos_add[:, :], 0.0).then_inc(pos_zero, 1)
                pool.memset(pos[:, :], 0.0).then_inc(pos_zero, 1)
                pool.memset(sum_lhs[:, :], 1.0).then_inc(const_c, 1)
                pool.memset(eps[:, :], EPS).then_inc(const_f, 1)
                pool.memset(mhalf[:, :], -0.5).then_inc(const_f, 1)
                pool.wait_ge(const_f, 2)
                pool.wait_ge(w_a, n_loads_a)

                def make_rstd(k, t, var, dst):
                    pool.tensor_tensor(ve[:, k, :], var, eps[0:C, :], ALU.add).then_inc(ve_ready[k], 1)
                    pool.wait_ge(ve_ready[k], t + 1)
                    return pool.tensor_tensor(dst, ve[:, k, :], mhalf[0:C, :], ALU.pow)

                def body(j, u, has):
                    if has(1):
                        t, _, u1 = tile_at(j, u, 1)
                        pool.wait_ge(mv2_ready, t + 1)
                        make_rstd(1, t, mv2[:, u1, 1:2], rstd[:, 1, u1:u1 + 1]).then_inc(rstd2_ready, 1)
                    if has(3):
                        t, _, u3 = tile_at(j, u, 3)
                        pool.wait_ge(mv1_ready, t + 1)
                        make_rstd(0, t, mv1[:, u3, 1:2], rstd[:, 0, u3:u3 + 1]).then_inc(rstd1_ready, 1)
                    if has(1):
                        t, _, u1 = tile_at(j, u, 1)
                        pool.wait_ge(mv3_ready, t + 1)
                        make_rstd(2, t, mv3[:, u1, 1:2], rstd[:, 2, u1:u1 + 1]).then_inc(rstd3_ready, 1)
                    if has(0):
                        t = tile_at(j, u, 0)[0]
                        pool.wait_ge(max_ready, t + 1)
                        pool.tensor_tensor(diag[0:C, :, :],
                                           nident[:, :].unsqueeze(1).to_broadcast([C, H, C]),
                                           mx[:, :].unsqueeze(2).to_broadcast([C, H, C]),
                                           ALU.mult).then_inc(diag_ready, 1)
                    if has(1):
                        t, _, u1 = tile_at(j, u, 1)
                        pool.wait_ge(h_ready, t + 1)
                        if late(t, 2):
                            pool.wait_ge(h1_ready, t - 1)
                        pool.tensor_tensor(hb[:, u1, :], h[:, u1, :], bo[:, :], ALU.add).then_inc(hb_ready, 1)

                steps(pool, body, NA, 3, 1)

            @block.vector
            def _(dve):
                dve.wait_ge(w_a, n_loads_a)
                dve.tensor_copy(mask_b[:, :], mask_f[:, :]).then_inc(mask_ready, 1)
                dve.tensor_copy(ln1_b_rep[:, :, :],
                                ln1_b[:, :].unsqueeze(2).to_broadcast([128, KP, C])).then_inc(rep_ready, 1)
                dve.memset(v_aug[:, :, :, :], 1.0).then_inc(rep_ready, 1)
                dve.wait_ge(bias_ps, 1)
                dve.tensor_tensor(lin_bias[:, :], ps_l[0:C, 0:D], lin_bias[:, :], ALU.add).then_inc(rep_ready, 1)
                dve.tensor_tensor(lin_w[:, :, :], lin_w[:, :, :],
                                  ln1_w[:, :].unsqueeze(2).to_broadcast([128, KP, D]),
                                  ALU.mult).then_inc(fold_ready, 1)
                dve.wait_ge(w_b, n_loads_rows)
                dve.tensor_tensor(pos_add[:, :], pos_add[:, :], pos[:, :], ALU.add).then_inc(pos_ready, 1)
                dve.wait_ge(pos_ready, 1)
                dve.wait_ge(rep_ready, 3)

                def normalise(t, j, u):
                    dve.wait_ge(pv_ps, t + 1)
                    pv = ps_o[0:C, 0:H * (DK + 1)].rearrange("p (h d) -> p h d", h=H)
                    dve.reciprocal(rden[:, :], pv[:, :, DK]).then_inc(rden_ready, 1)
                    dve.wait_ge(rden_ready, t + 1)
                    dve.tensor_tensor(o[:, :].rearrange("p (h d) -> p h d", h=H), pv[:, :, 0:DK],
                                      rden[:, :].unsqueeze(2).to_broadcast([C, H, DK]),
                                      ALU.mult).then_inc(o_ready, 1)

                def row_max(t, j, u):
                    dve.wait_ge(s_ps, t + 1)
                    dve.tensor_reduce(mx[:, :], ps_s[0:C, :, 0:HB * C].rearrange("p b (h k) -> p b h k", h=HB),
                                      AX, ALU.max).then_inc(max_ready, 1)

                def residual(t, j, u):
                    dve.wait_ge(wo_ps, t + 1)
                    dve.wait_ge(hb_ready, t + 1)
                    if late(t, 2):
                        dve.wait_ge(h1_stored[u], 16 * j)
                    dve.tensor_tensor(h1[:, u, :], ps_o[0:C, 0:D], hb[:, u, :], ALU.add).then_inc(h1_ready, 1)

                def stats1(t, j, u):
                    dve.wait_ge(x_loaded[u], 16 * (j + 1))
                    dve.bn_stats(st1[:, u, 0:6], xin[:, u, 0:PD // 2])
                    if late(t, 3):
                        dve.wait_ge(st2_ready, t - 1)
                    dve.bn_stats(st1[:, u, 6:12], xin[:, u, PD // 2:PD]).then_inc(st1_ready, 1)

                def aggregate(ready, mv, st, done, t, u):
                    if isinstance(t, int):
                        dve.wait_ge(ready, t + 1)
                    dve.bn_aggr(mv[:, u, :], st[:, u, :]).then_inc(done, 1)

                def norm1(t, j, u):
                    dve.wait_ge(rstd1_ready, t + 1)
                    if late(t, 2):
                        dve.wait_ge(xT_ps, t - 1)
                        dve.wait_ge(st3_ready, t - 1)
                    dve.tensor_scalar(xn[:, u, :], xin[:, u, :], mv1[:, u, 0:1], rstd[:, 0, u:u + 1],
                                      ALU.subtract, ALU.mult).then_inc(xn_ready, 1)

                def embed(t, j, u):
                    dve.wait_ge(lin_ps, t + 1)
                    dve.tensor_tensor(y[:, :], ps_l[0:C, 0:D], lin_bias[:, :], ALU.add).then_inc(y_ready, 1)
                    dve.wait_ge(y_ready, t + 1)
                    dve.bn_stats(st2[:, u, :], y[:, :]).then_inc(st2_ready, 1)

                def layer_norm2(t, j, u):
                    if not isinstance(t, int):
                        dve.wait_ge(st1_ready, t + 3)
                    dve.wait_ge(rstd2_ready, t + 1)
                    dve.tensor_scalar(yn[:, :], y[:, :], mv2[:, u, 0:1], rstd[:, 1, u:u + 1],
                                      ALU.subtract, ALU.mult).then_inc(yn_ready, 1)

                def tokens(t, j, u):
                    dve.wait_ge(yn_ready, t + 1)
                    dve.tensor_tensor(yw[:, :], yn[:, :], ln2_w[:, :], ALU.mult).then_inc(yw_ready, 1)
                    dve.wait_ge(yw_ready, t + 1)
                    dve.tensor_tensor(h[:, u, :], yw[:, :], pos_add[:, :], ALU.add).then_inc(h_ready, 1)
                    dve.wait_ge(h_ready, t + 1)
                    dve.bn_stats(st3[:, u, :], h[:, u, :]).then_inc(st3_ready, 1)

                def norm3(t, j, u):
                    dve.wait_ge(rstd3_ready, t + 1)
                    dve.tensor_scalar(hn[:, :], h[:, u, :], mv3[:, u, 0:1], rstd[:, 2, u:u + 1],
                                      ALU.subtract, ALU.mult).then_inc(hn_ready, 1)

                def expand(t, j, u):
                    mask = headmask[:, :].unsqueeze(2).to_broadcast([128, HC, C])
                    dve.wait_ge(v_ps, t + 1)
                    dve.tensor_tensor(v_aug[:, u, :, 0:DK], ps_l[0:C, 0:D].rearrange("p (h d) -> p h d", h=H),
                                      bv[:, :].rearrange("p (h d) -> p h d", h=H), ALU.add).then_inc(v_ready, 1)
                    dve.wait_ge(qk_ready, t + 1)
                    for c in range(KD):
                        i = dve.tensor_tensor(k_exp[:, c, :, :], kT[:, c, :].unsqueeze(1).to_broadcast([128, HC, C]),
                                              mask, ALU.mult)
                    i.then_inc(kexp_ready, 1)
                    for c in range(KD):
                        i = dve.tensor_tensor(q_exp[:, c, :, :], qT[:, c, :].unsqueeze(1).to_broadcast([128, HC, C]),
                                              mask, ALU.mult)
                    i.then_inc(qexp_ready, 1)

                def body(j, u, has):
                    t1, u1 = tile_at(j, u, 1)[::2]
                    t3, u3 = tile_at(j, u, 3)[::2]
                    if has(1):
                        embed(*tile_at(j, u, 1))
                    if has(3):
                        stats1(*tile_at(j, u, 3))
                    if has(1):
                        aggregate(st2_ready, mv2, st2, mv2_ready, t1, u1)
                    if has(-1):
                        normalise(*tile_at(j, u, -1))
                    if has(1):
                        layer_norm2(*tile_at(j, u, 1))
                    if has(3):
                        aggregate(st1_ready, mv1, st1, mv1_ready, t3, u3)
                    if has(1):
                        tokens(*tile_at(j, u, 1))
                    if has(3):
                        norm1(*tile_at(j, u, 3))
                    if has(1):
                        aggregate(st3_ready, mv3, st3, mv3_ready, t1, u1)
                    if has(0):
                        row_max(*tile_at(j, u, 0))
                    if has(1):
                        norm3(*tile_at(j, u, 1))
                    if has(-1):
                        residual(*tile_at(j, u, -1))
                    if has(1):
                        expand(*tile_at(j, u, 1))

                steps(dve, body, NA, 3, 1)

            @block.scalar
            def _(act):
                def copy_xT(t, j, u):
                    act.wait_ge(xT_ps, t + 1)
                    if late(t, 1):
                        act.wait_ge(lin_ps, t)
                    act.activation(xT[:, 0:4, :], ps_x[:, 0:4 * C].rearrange("p (k c) -> p k c", k=4), ACT.Copy)
                    act.activation(xT[:, 4:KP, :], ps_y[:, 0:2 * C].rearrange("p (k c) -> p k c", k=2),
                                   ACT.Copy).then_inc(xT_ready, 1)

                def copy_oT(t, j, u):
                    act.wait_ge(oT_ps, t + 1)
                    act.activation(oT[:, :, :], ps_o[:, 0:KD * C].rearrange("p (k c) -> p k c", k=KD),
                                   ACT.Copy).then_inc(oT_ready, 1)

                def copy_hnT(t, j, u):
                    act.wait_ge(hnT_ps, t + 1)
                    act.activation(hnT[:, :, :], ps_y[:, 0:KD * C].rearrange("p (k c) -> p k c", k=KD),
                                   ACT.Copy).then_inc(hnT_ready, 1)

                def exp_scores(t, j, u):
                    act.wait_ge(st_ps, t + 1)
                    for b in range(4):
                        i = act.activation(pT[:, b * HB:(b + 1) * HB, :],
                                           ps_s[0:C, b, 0:HB * C].rearrange("p (h q) -> p h q", h=HB),
                                           ACT.Exp, scale=float(DK) ** -0.5)
                    i.then_inc(p_ready, 1)

                def copy_qk(t, j, u):
                    act.wait_ge(qk_ps, t + 1)
                    if late(t, 1):
                        act.wait_ge(qexp_ready, t)
                    for c in range(KD):
                        act.activation(kT[:, c, :], ps_x[:, (KD + c) * C:(KD + c + 1) * C], ACT.Identity,
                                       bias=bk[:, c:c + 1])
                    for c in range(KD):
                        i = act.activation(qT[:, c, :], ps_x[:, c * C:(c + 1) * C], ACT.Identity,
                                           bias=bq[:, c:c + 1])
                    i.then_inc(qk_ready, 1)
                    act.wait_ge(qk_ready, t + 1)
                    act.activation(qTb[:, :, :], qT[:, :, :], ACT.Copy).then_inc(qb_ready, 1)

                def body(j, u, has):
                    if has(-1):
                        copy_oT(*tile_at(j, u, -1))
                    if has(1):
                        copy_hnT(*tile_at(j, u, 1))
                    if has(0):
                        exp_scores(*tile_at(j, u, 0))
                    if has(1):
                        copy_qk(*tile_at(j, u, 1))
                    if has(2):
                        copy_xT(*tile_at(j, u, 2))

                for dst, src in loads_b:
                    act.dma_start(dst, src).then_inc(w_b2, 16)
                act.wait_ge(w_a, n_loads_a)
                steps(act, body, NA, 3, 1)
                act.wait_ge(w_b2, 16 * len(loads_b))

            @block.tensor
            def _(pe):
                pe.wait_ge(w_a, n_loads_a)
                pe.wait_ge(rep_ready, 1)
                for k in range(KP):
                    i = pe.matmul(ps_l[0:C, 0:D], ln1_b_rep[:, k, :], lin_w[:, k, :], start=k == 0, stop=k == KP - 1)
                i.then_inc(bias_ps, 1)
                pe.wait_ge(mask_moved, 16 * (H // HB + 1))

                def transpose_x(t, j, u):
                    pe.wait_ge(xn_ready, t + 1)
                    if late(t, 1):
                        pe.wait_ge(qk_ready, t)
                    for k in range(KP):
                        dst = ps_x[:, k * C:(k + 1) * C] if k < 4 else ps_y[:, (k - 4) * C:(k - 3) * C]
                        i = pe.transpose(dst, xn[:, u, k * 128:(k + 1) * 128], ident[0:C, 0:C])
                    i.then_inc(xT_ps, 1)

                def transpose_o(t, j, u):
                    pe.wait_ge(o_ready, t + 1)
                    for k in range(KD):
                        i = pe.transpose(ps_o[:, k * C:(k + 1) * C], o[:, k * 128:(k + 1) * 128], ident[0:C, 0:C])
                    i.then_inc(oT_ps, 1)

                def scores_for_max(t, j, u):
                    pe.wait_ge(kexp_ready, t + 1)
                    pe.wait_ge(qb_ready, t + 1)
                    if late(t, 1):
                        pe.wait_ge(p_ready, t)
                    for b in range(4):
                        c, s0 = b // 2, (b % 2) * HB
                        pe.matmul(ps_s[0:C, b, 0:HB * C], qTb[:, c, :], k_exp[:, c, s0:s0 + HB, :],
                                  start=True, stop=False)
                        i = pe.matmul(ps_s[0:C, b, 0:HB * C], mask_b[:, 0:C], mask_b[:, 2 * C:2 * C + HB * C],
                                      start=False, stop=True)
                    i.then_inc(s_ps, 1)

                def project_o(t, j, u):
                    pe.wait_ge(oT_ready, t + 1)
                    for k in range(KD):
                        i = pe.matmul(ps_o[0:C, 0:D], oT[:, k, :], wo[:, k, :], start=k == 0, stop=k == KD - 1)
                    i.then_inc(wo_ps, 1)

                def linear(t, j, u):
                    pe.wait_ge(xT_ready, t + 1)
                    if late(t, 1):
                        pe.wait_ge(v_ready, t)
                    else:
                        pe.wait_ge(fold_ready, 1)
                    for k in range(KP):
                        i = pe.matmul(ps_l[0:C, 0:D], xT[:, k, :], lin_w[:, k, :], start=k == 0, stop=k == KP - 1)
                    i.then_inc(lin_ps, 1)

                def scores(t, j, u):
                    pe.wait_ge(qexp_ready, t + 1)
                    pe.wait_ge(max_ready, t + 1)
                    for b in range(4):
                        c, s0 = b // 2, (b % 2) * HB
                        pe.matmul(ps_s[0:C, b, 0:HB * C], kT[:, c, :], q_exp[:, c, s0:s0 + HB, :],
                                  start=True, stop=False)

                def transpose_hn(t, j, u):
                    pe.wait_ge(hn_ready, t + 1)
                    for k in range(KD):
                        i = pe.transpose(ps_y[:, k * C:(k + 1) * C], hn[:, k * 128:(k + 1) * 128], ident[0:C, 0:C])
                    i.then_inc(hnT_ps, 1)

                def shift(t, j, u):
                    pe.wait_ge(diag_ready, t + 1)
                    for b in range(4):
                        i = pe.matmul(ps_s[0:C, b, 0:HB * C], sum_lhs[:, :], diag[:, b * HB:(b + 1) * HB, :],
                                      start=False, stop=True)
                    i.then_inc(st_ps, 1)

                def project_qkv(t, j, u):
                    pe.wait_ge(hnT_ready, t + 1)
                    for w, at in ((wq, 0), (wk, KD)):
                        for m in range(KD):
                            for k in range(KD):
                                i = pe.matmul(ps_x[:, (at + m) * C:(at + m + 1) * C],
                                              w[:, k, m * 128:(m + 1) * 128], hnT[:, k, :],
                                              start=k == 0, stop=k == KD - 1)
                    i.then_inc(qk_ps, 1)
                    for k in range(KD):
                        i = pe.matmul(ps_l[0:C, 0:D], hnT[:, k, :], wv[:, k, :], start=k == 0, stop=k == KD - 1)
                    i.then_inc(v_ps, 1)

                def weighted_values(t, j, u):
                    pe.wait_ge(p_ready, t + 1)
                    pe.wait_ge(v_ready, t + 1)
                    if late(t, 1):
                        pe.wait_ge(h1_ready, t)
                    for n in range(H):
                        i = pe.matmul(ps_o[0:C, n * (DK + 1):(n + 1) * (DK + 1)], pT[:, n, :],
                                      v_aug[:, u, n, :], start=True, stop=True)
                    i.then_inc(pv_ps, 1)

                def body(j, u, has):
                    if has(0):
                        scores_for_max(*tile_at(j, u, 0))
                    if has(-1):
                        transpose_o(*tile_at(j, u, -1))
                        project_o(*tile_at(j, u, -1))
                    if has(0):
                        scores(*tile_at(j, u, 0))
                    if has(1):
                        transpose_hn(*tile_at(j, u, 1))
                    if has(0):
                        shift(*tile_at(j, u, 0))
                    if has(1):
                        project_qkv(*tile_at(j, u, 1))
                    if has(2):
                        transpose_x(*tile_at(j, u, 2))
                        linear(*tile_at(j, u, 2))
                    if has(0):
                        weighted_values(*tile_at(j, u, 0))

                steps(pe, body, NA, 3, 1)
        with ExitStack() as cb:
            def sbb(name, shape, dt=F32):
                return cb.enter_context(nc.sbuf_tensor(name, shape, dt))

            def pb(name, shape):
                return cb.enter_context(nc.psum_tensor(name, shape, F32))

            hx = sbb("hx", [128, 4, D])
            hxb = sbb("hxb", [128, 2, D])
            stf = sbb("stf", [128, 2, 6])
            mvf = sbb("mvf", [128, 2, 2])
            vef = sbb("vef", [128, 1])
            rstdf = sbb("rstdf", [128, 2])
            hf = sbb("hf", [128, D])
            hfT = sbb("hfT", [128, KD, 128])
            sims = sbb("sims", [128, 2, 2, PH, NK])
            gate = sbb("gate", [128, 2, KF, 128])
            gate_t = sbb("gate_t", [128, 2, KF, 128])
            upp = sbb("upp", [128, 2, KF, 128])
            act_a = sbb("act_a", [128, KF, 128])
            hid = sbb("hid", [128, KF, 128])
            de_t = sbb("de_t", [128, NE])
            silu2 = sbb("silu2", [128, NE])
            top = sbb("top", [128, 2, PH, T8])
            grid = sbb("grid", [128, PH, T8, T8])
            best = sbb("best", [128, PH, T8])
            rel = sbb("rel", [128, PH, T8])
            erel = sbb("erel", [128, PH, T8])
            neg_m = sbb("neg_m", [128, PH])
            zsum = sbb("zsum", [128, PH])
            rz = sbb("rz", [128, PH])
            pair = sbb("pair", [128, PH, XR, NK])
            epair = sbb("epair", [128, PH, XR, NK])
            picked = sbb("picked", [128, PH])
            rest = sbb("rest", [128, PH])
            restw = sbb("restw", [128, PH])
            rest1 = sbb("rest1", [128, 1])
            coef = sbb("coef", [128, 2, NE])
            wgt = sbb("wgt", [128, NE])
            wT = sbb("wT", [128, NE // 128, 128])
            res = sbb("res", [128, 2, D])

            ps_m = pb("ps_m", [128, 512])
            ps_out = pb("ps_out", [128, 512])
            ps_e = pb("ps_e", [128, 2, 512])
            ps_g = pb("ps_g", [128, 2, 512])
            ps_u = pb("ps_u", [128, 2, 512])

            names = ("w_loaded w2_ready simw_ps simw_ready h_loaded0 h_loaded1 h_loaded2 h_loaded3 "
                     "stf_ready mvf_ready vef_ready rstdf_ready hf_ready hxb_ready hfT_ps hfT_ready "
                     "sim_ps sims_ready e_ps e_tanh gate_ps up_ps gate_ready gate_t_ready up_ready "
                     "silu_ready top_ready grid_ready best_ready rel_ready negm_ready erel_ready z_ready "
                     "rz_ready pair_ready epair_ready picked_ready act_ready hid_ready coef_step "
                     "rest_ready restw_ready rest1_ready coef_ready wgt_ready wT_ps wT_ready out_ps "
                     "res_ready stored0 stored1").split()
            q = {n: cb.enter_context(nc.semaphore("b_" + n)) for n in names}
            stored = [q["stored0"], q["stored1"]]
            h_loaded = [q[f"h_loaded{i}"] for i in range(4)]
            block = cb.enter_context(nc.Block())

            def rows_at(t):
                return N - 128 if isinstance(t, int) and t == NB - 1 else t * 128

            @block.sync
            def _(sp):
                def load_h(t, j, u):
                    if late(t, 2):
                        sp.wait_ge(q["hf_ready"], t - 1)
                        sp.wait_ge(q["hxb_ready"], t - 1)
                    sp.dma_start(hx[:, u, :], h1_dram[bass.ds(rows_at(t), 128), :]).then_inc(h_loaded[u], 16)

                def store(t, j, u):
                    sp.wait_ge(q["res_ready"], t + 1)
                    new = N - (NB - 1) * 128 if isinstance(t, int) and t == NB - 1 else 128
                    sp.dma_start(out[bass.ds(rows_at(t) + 128 - new, new), :],
                                 res[128 - new:128, u, :]).then_inc(stored[u], 16)

                def body(j, u, has):
                    if has(2):
                        load_h(*tile_at(j, u, 2))
                    if has(-1):
                        store(*tile_at(j, u, -1))

                steps(sp, body, NB, 2, 1)
                for u in (0, 1):
                    sp.wait_ge(stored[u], 16 * ((NB + 1 - u) // 2))

            @block.gpsimd
            def _(pool):
                def body(j, u, has):
                    if has(1):
                        t, tj, tu = tile_at(j, u, 1)
                        pool.wait_ge(q["mvf_ready"], t + 1)
                        pool.tensor_tensor(vef[:, :], mvf[:, tu, 1:2], eps[:, :], ALU.add).then_inc(q["vef_ready"], 1)
                        pool.wait_ge(q["vef_ready"], t + 1)
                        pool.tensor_tensor(rstdf[:, tu:tu + 1], vef[:, :], mhalf[:, :],
                                           ALU.pow).then_inc(q["rstdf_ready"], 1)
                        if late(t, 2):
                            pool.wait_ge(q["res_ready"], t - 1)
                        pool.tensor_tensor(hxb[:, tu, :], hx[:, tu, :], bd[:, :], ALU.add).then_inc(q["hxb_ready"], 1)

                steps(pool, body, NB, 2, 1)

            @block.vector
            def _(dve):
                dve.tensor_scalar(bg_half[:, :], bg[:, :], 0.5, None, ALU.mult).then_inc(q["w2_ready"], 1)
                dve.wait_ge(q["simw_ps"], 1)
                dve.tensor_copy(simw[:, :, :], ps_g[:, :, :]).then_inc(q["simw_ready"], 1)

                def stats(t, j, u):
                    dve.wait_ge(h_loaded[u], 16 * (j + 1))
                    dve.bn_stats(stf[:, u, :], hx[:, u, :]).then_inc(q["stf_ready"], 1)

                def aggregate(t, j, u):
                    if isinstance(t, int):
                        dve.wait_ge(q["stf_ready"], t + 1)
                    dve.bn_aggr(mvf[:, u, :], stf[:, u, :]).then_inc(q["mvf_ready"], 1)

                def norm(t, j, u):
                    dve.wait_ge(q["rstdf_ready"], t + 1)
                    if late(t, 1):
                        dve.wait_ge(q["hfT_ps"], t)
                    dve.tensor_scalar(hf[:, :], hx[:, u, :], mvf[:, u, 0:1], rstdf[:, u:u + 1],
                                      ALU.subtract, ALU.mult).then_inc(q["hf_ready"], 1)

                def expert_silu(t, j, u):
                    if not isinstance(t, int):
                        dve.wait_ge(q["stf_ready"], t + 2)
                    dve.wait_ge(q["sims_ready"], t + 1)
                    if late(t, 1):
                        dve.wait_ge(q["wgt_ready"], t)
                    dve.wait_ge(q["e_tanh"], t + 1)
                    dve.scalar_tensor_tensor(silu2[:, :], de_t[:, :], 1.0, ps_e[:, :, :].rearrange("p a b -> p (a b)"),
                                             ALU.add, ALU.mult).then_inc(q["silu_ready"], 1)

                def top_keys(t, j, u):
                    for p in range(2):
                        for n in range(PH):
                            i = dve.max(top[:, p, n, :], sims[:, u, p, n, :])
                    i.then_inc(q["top_ready"], 1)

                def top_pairs(t, j, u):
                    dve.wait_ge(q["top_ready"], t + 1)
                    dve.tensor_tensor(grid[:, :, :, :],
                                      top[:, 0, :, :].unsqueeze(3).to_broadcast([128, PH, T8, T8]),
                                      top[:, 1, :, :].unsqueeze(2).to_broadcast([128, PH, T8, T8]),
                                      ALU.add).then_inc(q["grid_ready"], 1)

                def best_pairs(t, j, u):
                    for n in range(PH):
                        i = dve.max(best[:, n, :], grid[:, n, :, :].rearrange("p a b -> p (a b)"))
                    i.then_inc(q["best_ready"], 1)

                def relative(t, j, u):
                    dve.wait_ge(q["best_ready"], t + 1)
                    dve.tensor_scalar(neg_m[:, :], best[:, :, 0], -1.0, None, ALU.mult).then_inc(q["negm_ready"], 1)
                    dve.tensor_tensor(rel[:, :, :], best[:, :, :],
                                      best[:, :, 0:1].to_broadcast([128, PH, T8]),
                                      ALU.subtract).then_inc(q["rel_ready"], 1)

                def normaliser(t, j, u):
                    dve.wait_ge(q["erel_ready"], t + 1)
                    dve.tensor_reduce(zsum[:, :], erel[:, :, :], AX, ALU.add).then_inc(q["z_ready"], 1)
                    dve.wait_ge(q["z_ready"], t + 1)
                    dve.reciprocal(rz[:, :], zsum[:, :]).then_inc(q["rz_ready"], 1)

                def pair_sums(t, j, u, n):
                    if n == 2:
                        dve.wait_ge(q["grid_ready"], t + 1)
                    dve.tensor_tensor(pair[:, n, :, :],
                                      sims[:, u, 0, n, 0:XR].unsqueeze(2).to_broadcast([128, XR, NK]),
                                      sims[:, u, 1, n, :].unsqueeze(1).to_broadcast([128, XR, NK]),
                                      ALU.add).then_inc(q["pair_ready"], 1)

                def pick(t, j, u, n):
                    dve.wait_ge(q["epair_ready"], PH * t + n + 1)
                    dve.scalar_tensor_tensor(pair[:, n, :, :].rearrange("p a b -> p (a b)"),
                                             pair[:, n, :, :].rearrange("p a b -> p (a b)"), best[:, n, T8 - 1:T8],
                                             epair[:, n, :, :].rearrange("p a b -> p (a b)"),
                                             ALU.is_ge, ALU.mult, accum_out=picked[:, n:n + 1]).then_inc(q["picked_ready"], 1)

                def combine(t, j, u, n):
                    dve.wait_ge(q["picked_ready"], PH * t + n + 1)
                    flat = pair[:, n, :, :].rearrange("p a b -> p (a b)")
                    if n == 0:
                        dve.wait_ge(q["rz_ready"], t + 1)
                        dve.tensor_scalar(coef[:, 0, :], flat, rz[:, 0:1], None, ALU.mult).then_inc(q["coef_step"], 1)
                    else:
                        dve.wait_ge(q["coef_step"], PH * t + n)
                        dve.scalar_tensor_tensor(coef[:, n % 2, :], flat, rz[:, n:n + 1], coef[:, 1 - n % 2, :],
                                                 ALU.mult, ALU.add).then_inc(q["coef_step"], 1)

                def rest_of(t, j, u):
                    dve.wait_ge(q["picked_ready"], PH * t + PH)
                    dve.tensor_tensor(rest[:, :], zsum[:, :], picked[:, :], ALU.subtract).then_inc(q["rest_ready"], 1)
                    dve.wait_ge(q["rest_ready"], t + 1)
                    dve.tensor_tensor(restw[:, :], rest[:, :], rz[:, :], ALU.mult).then_inc(q["restw_ready"], 1)
                    dve.wait_ge(q["restw_ready"], t + 1)
                    dve.tensor_reduce(rest1[:, :], restw[:, :], AX, ALU.add).then_inc(q["rest1_ready"], 1)

                def weights(t, j, u):
                    last = (PH - 1) % 2
                    dve.wait_ge(q["rest1_ready"], t + 1)
                    dve.wait_ge(q["coef_step"], PH * (t + 1))
                    dve.tensor_tensor(coef[:, last, NE - 1:NE], coef[:, last, NE - 1:NE], rest1[:, :],
                                      ALU.add).then_inc(q["coef_ready"], 1)
                    dve.wait_ge(q["coef_ready"], t + 1)
                    dve.scalar_tensor_tensor(wgt[:, :], silu2[:, :], 0.5, coef[:, last, :],
                                             ALU.mult, ALU.mult).then_inc(q["wgt_ready"], 1)

                def mlp_a(t, j, u):
                    dve.wait_ge(q["gate_t_ready"], t + 1)
                    dve.scalar_tensor_tensor(act_a[:, :, :], gate_t[:, u, :, :], 1.0, gate[:, u, :, :],
                                             ALU.add, ALU.mult).then_inc(q["act_ready"], 1)

                def mlp_b(t, j, u):
                    dve.wait_ge(q["act_ready"], t + 1)
                    dve.wait_ge(q["up_ready"], t + 1)
                    if late(t, 1):
                        dve.wait_ge(q["out_ps"], t)
                    dve.scalar_tensor_tensor(hid[:, :, :], act_a[:, :, :], 0.5, upp[:, u, :, :],
                                             ALU.mult, ALU.mult).then_inc(q["hid_ready"], 1)

                def result(t, j, u):
                    dve.wait_ge(q["hxb_ready"], t + 1)
                    dve.wait_ge(q["out_ps"], t + 1)
                    if late(t, 2):
                        dve.wait_ge(stored[u], 16 * j)
                    dve.tensor_tensor(res[:, u, :], ps_out[:, 0:D], hxb[:, u, :], ALU.add).then_inc(q["res_ready"], 1)

                def body(j, u, has):
                    now, nxt, prv = tile_at(j, u, 0), tile_at(j, u, 1), tile_at(j, u, -1)
                    if has(1):
                        stats(*nxt)
                    if has(0):
                        expert_silu(*now)
                    if has(1):
                        aggregate(*nxt)
                    if has(0):
                        top_keys(*now)
                    if has(1):
                        norm(*nxt)
                    if has(0):
                        pair_sums(*now, 0)
                        top_pairs(*now)
                        pair_sums(*now, 1)
                        pair_sums(*now, 2)
                        best_pairs(*now)
                        relative(*now)
                        pair_sums(*now, 3)
                        mlp_a(*now)
                    if has(-1):
                        result(*prv)
                    if has(0):
                        mlp_b(*now)
                        normaliser(*now)
                        pick(*now, 0)
                        pick(*now, 1)
                        combine(*now, 0)
                        pick(*now, 2)
                        combine(*now, 1)
                        pick(*now, 3)
                        combine(*now, 2)
                        rest_of(*now)
                        combine(*now, 3)
                        weights(*now)

                steps(dve, body, NB, 2, 1)

            @block.scalar
            def _(act):
                act.wait_ge(q["w2_ready"], 1)

                def front(t, j, u):
                    act.wait_ge(q["hfT_ps"], t + 1)
                    act.activation(hfT[:, :, :], ps_m[:, 0:D].rearrange("p (k c) -> p k c", k=KD),
                                   ACT.Copy).then_inc(q["hfT_ready"], 1)
                    act.wait_ge(q["sim_ps"], t + 1)
                    act.activation(sims[:, u, :, :, :].rearrange("p a b c -> p (a b c)"), ps_m[:, :],
                                   ACT.Copy).then_inc(q["sims_ready"], 1)

                def gate_up(t, j, u):
                    act.wait_ge(q["gate_ps"], t + 1)
                    for m in range(KF):
                        i = act.activation(gate[:, u, m, :], ps_g[:, m // 4, (m % 4) * 128:(m % 4 + 1) * 128],
                                           ACT.Identity, bias=bg[:, m:m + 1])
                    i.then_inc(q["gate_ready"], 1)
                    act.wait_ge(q["up_ps"], t + 1)
                    for m in range(KF):
                        i = act.activation(upp[:, u, m, :], ps_u[:, m // 4, (m % 4) * 128:(m % 4 + 1) * 128],
                                           ACT.Identity, bias=bu[:, m:m + 1])
                    i.then_inc(q["up_ready"], 1)
                    act.wait_ge(q["gate_ready"], t + 1)
                    act.activation(gate_t[:, u, :, :], gate[:, u, :, :], ACT.Tanh, scale=0.5).then_inc(q["gate_t_ready"], 1)

                def expert_tanh(t, j, u):
                    act.wait_ge(q["e_ps"], t + 1)
                    if late(t, 1):
                        act.wait_ge(q["silu_ready"], t)
                    act.activation(de_t[:, :], ps_e[:, :, :].rearrange("p a b -> p (a b)"), ACT.Tanh,
                                   scale=0.5).then_inc(q["e_tanh"], 1)

                def exps(t, j, u):
                    act.wait_ge(q["rel_ready"], t + 1)
                    act.activation(erel[:, :, :], rel[:, :, :], ACT.Exp).then_inc(q["erel_ready"], 1)
                    act.wait_ge(q["negm_ready"], t + 1)
                    for n in range(PH):
                        act.wait_ge(q["pair_ready"], PH * t + n + 1)
                        act.activation(epair[:, n, :, :], pair[:, n, :, :], ACT.Exp,
                                       bias=neg_m[:, n:n + 1]).then_inc(q["epair_ready"], 1)

                def copy_wT(t, j, u):
                    act.wait_ge(q["wT_ps"], t + 1)
                    if late(t, 1):
                        act.wait_ge(q["out_ps"], t)
                    act.activation(wT[:, :, :].rearrange("p a b -> p (a b)"),
                                   ps_g[:, :, :].rearrange("p a b -> p (a b)"), ACT.Copy).then_inc(q["wT_ready"], 1)

                def body(j, u, has):
                    now, nxt = tile_at(j, u, 0), tile_at(j, u, 1)
                    if has(1):
                        front(*nxt)
                    if has(0):
                        exps(*now)
                    if has(1):
                        expert_tanh(*nxt)
                        gate_up(*nxt)
                    if has(0):
                        copy_wT(*now)

                steps(act, body, NB, 2, 1)

            @block.tensor
            def _(pe):
                for k in range(KD):
                    for n in range(2 * PH):
                        i = pe.matmul(ps_g[:, k, n * NK:(n + 1) * NK], wqf[:, n, k * 128:(k + 1) * 128],
                                      keys[:, n, :], start=True, stop=True)
                i.then_inc(q["simw_ps"], 1)
                pe.wait_ge(q["simw_ready"], 1)

                def transpose_h(t, j, u):
                    pe.wait_ge(q["hf_ready"], t + 1)
                    if late(t, 1):
                        pe.wait_ge(q["sims_ready"], t)
                    for k in range(KD):
                        i = pe.transpose(ps_m[:, k * 128:(k + 1) * 128], hf[:, k * 128:(k + 1) * 128], ident[:, :])
                    i.then_inc(q["hfT_ps"], 1)

                def similarities(t, j, u):
                    pe.wait_ge(q["hfT_ready"], t + 1)
                    for k in range(KD):
                        i = pe.matmul(ps_m[:, :], hfT[:, k, :], simw[:, k, :], start=k == 0, stop=k == KD - 1)
                    i.then_inc(q["sim_ps"], 1)

                def experts(t, j, u):
                    if late(t, 1):
                        pe.wait_ge(q["silu_ready"], t)
                    for b in range(2):
                        for k in range(KD):
                            i = pe.matmul(ps_e[:, b, :], hfT[:, k, :], down[:, k, b * 512:(b + 1) * 512],
                                          start=k == 0, stop=k == KD - 1)
                    i.then_inc(q["e_ps"], 1)

                def gate_up(t, j, u):
                    if late(t, 2):
                        pe.wait_ge(q["wT_ready"], t - 1)
                    for ps, w, done in ((ps_g, wg, q["gate_ps"]), (ps_u, wu, q["up_ps"])):
                        if ps is ps_u and late(t, 1):
                            pe.wait_ge(q["up_ready"], t)
                        for m in range(KF):
                            for k in range(KD):
                                i = pe.matmul(ps[:, m // 4, (m % 4) * 128:(m % 4 + 1) * 128],
                                              w[:, k, m * 128:(m + 1) * 128], hfT[:, k, :],
                                              start=k == 0, stop=k == KD - 1)
                        i.then_inc(done, 1)

                def mlp_out(t, j, u):
                    pe.wait_ge(q["hid_ready"], t + 1)
                    if late(t, 1):
                        pe.wait_ge(q["res_ready"], t)
                    for m in range(KF):
                        pe.matmul(ps_out[:, 0:D], hid[:, m, :], wd[:, m, :], start=m == 0, stop=False)

                def transpose_w(t, j, u, has_next):
                    pe.wait_ge(q["wgt_ready"], t + 1)
                    if has_next:
                        pe.wait_ge(q["gate_ready"], t + 2)
                    for m in range(NE // 128):
                        i = pe.transpose(ps_g[:, m // 4, (m % 4) * 128:(m % 4 + 1) * 128],
                                         wgt[:, m * 128:(m + 1) * 128], ident[:, :])
                    i.then_inc(q["wT_ps"], 1)

                def experts_out(t, j, u):
                    pe.wait_ge(q["wT_ready"], t + 1)
                    for m in range(NE // 128):
                        i = pe.matmul(ps_out[:, 0:D], wT[:, m, :], up[:, m, :], start=False, stop=m == NE // 128 - 1)
                    i.then_inc(q["out_ps"], 1)

                def body(j, u, has):
                    now, nxt = tile_at(j, u, 0), tile_at(j, u, 1)
                    if has(1):
                        transpose_h(*nxt)
                        similarities(*nxt)
                        experts(*nxt)
                        gate_up(*nxt)
                    if has(0):
                        mlp_out(*now)
                        transpose_w(*now, has(1))
                        experts_out(*now)

                steps(pe, body, NB, 2, 1)


_WEIGHTS = None


def kernel(**inputs):
    import numpy as np
    import concourse.bacc as bacc
    from concourse.bass_utils import run_bass_kernel_spmd

    a = {k.replace("L0_", ""): np.asarray(v) for k, v in inputs.items()}

    def rows(w):
        return np.ascontiguousarray(w.reshape(-1, 128, w.shape[1]).transpose(1, 0, 2))

    def cols(b):
        return np.ascontiguousarray(b.reshape(-1, 128).T)

    n = IMG // P
    patches = a["x"].reshape(B, CH, n, P, n, P).transpose(0, 2, 4, 3, 5, 1).reshape(B, NP_, PD)
    x = np.zeros((NA, C, PD), np.float32)
    for t in range(NA):
        for g in range(G):
            x[t, g * S + 1:(g + 1) * S] = patches[min(G * t, B - G) + g]

    image = np.zeros((G, C), np.float32)
    for g in range(G):
        image[g, g * S:(g + 1) * S] = 1.0
    image_q = image.copy()
    image_q[0, R] = 1.0
    ones = np.ones((1, C), np.float32)
    far, near_k, near_q = -BIG * ones, BIG * image, BIG * image_q
    mask = np.concatenate([
        np.concatenate([ones, image_q]), np.concatenate([ones, image]),
        np.tile(np.concatenate([far, near_k]), (1, HB)), np.tile(np.concatenate([far, near_q]), (1, HB)),
    ], axis=1)
    feeds = {
        "x": x,
        "ident": np.eye(128, dtype=np.float32),
        "nident": -np.eye(C, dtype=np.float32),
        "headmask": np.kron(np.eye(HC, dtype=np.float32), np.ones((DK, 1), np.float32)),
        "mask": mask,
        "ln1_w": cols(a["tok_ln1_w"]), "ln1_b": cols(a["tok_ln1_b"]),
        "lin_w": rows(a["tok_lin_w"]), "lin_b": a["tok_lin_b"][None],
        "ln2_w": a["tok_ln2_w"][None], "ln2_b": a["tok_ln2_b"][None],
        "cls": a["tok_cls_token"][0], "pos": a["tok_pos_embedding"][0],
        "wq": rows(a["attn_Wq"].T), "wk": rows(a["attn_Wk"].T), "wv": rows(a["attn_Wv"].T),
        "wo": rows(a["attn_Wo"].T),
        "bq": cols(a["attn_bq"]), "bk": cols(a["attn_bk"]),
        "bv": a["attn_bv"][None], "bo": a["attn_bo"][None],
        "wg": rows(a["ffn_Wg"]), "wu": rows(a["ffn_Wu"]), "wd": rows(a["ffn_Wd"]),
        "bg": cols(a["ffn_bg"]), "bu": cols(a["ffn_bu"]), "bd": a["ffn_bd"][None],
        "wqf": np.ascontiguousarray(a["ffn_Wq"].reshape(D, 2 * PH, RET).transpose(2, 1, 0)),
        "keys": np.ascontiguousarray(a["ffn_keys"].transpose(3, 2, 0, 1).reshape(RET, 2 * PH, NK)),
        "down": rows(a["ffn_down_embed"].T), "up": rows(a["ffn_up_embed"]),
    }
    feeds = {f"in_{k}": np.ascontiguousarray(v) for k, v in feeds.items()}
    nc = bacc.Bacc("TRN2", target_bir_lowering=False, num_devices=1)
    args = {k[3:]: nc.dram_tensor(k, v.shape, F32, kind="ExternalInput").ap() for k, v in feeds.items()}
    out = nc.dram_tensor("out", (N, D), F32, kind="ExternalOutput").ap()
    h1_dram = nc.dram_tensor("h1_dram", (N, D), F32, kind="Internal").ap()
    vit_tower(nc, args, out, h1_dram)
    r = run_bass_kernel_spmd(nc, [feeds], core_ids=[0])
    return r.results[0]["out"].reshape(B, S, D)
```

```python
from contextlib import ExitStack

import concourse.bass as bass
from concourse import mybir

F32 = mybir.dt.float32
BF16 = mybir.dt.bfloat16
ALU = mybir.AluOpType
ACT = mybir.ActivationFunctionType
AX = mybir.AxisListType.X

B, CH, IMG, P = 64, 3, 96, 16
NP_ = (IMG // P) ** 2
S = NP_ + 1
PD = P * P * CH
D = 256
H, DK = 16, 16
G = 3
R = G * S
C = R + 1
NA = -(-B // G)
KP = PD // 128
KD = D // 128
HC = H // KD
HB = H // 4
N = B * S
NB = -(-N // 128)
F = 1024
KF = F // 128
PH, NK, RET = 4, 64, 64
NE = 1024
XR = NE // NK
T8 = 8
EPS = 1e-5
BIG = 65536.0


def late(t, n):
    return not isinstance(t, int) or t >= n


def steps(engine, body, n, ahead, behind):
    first = -ahead
    lo = 4
    hi = n - ahead
    hi -= (hi - lo) % 2
    for t in range(first, lo):
        body(t // 2, t % 2, lambda k, t=t: 0 <= t + k < n)
    with engine.Fori(lo // 2, hi // 2) as j:
        for u in (0, 1):
            body(j, u, lambda k: True)
    for t in range(hi, n + behind):
        body(t // 2, t % 2, lambda k, t=t: 0 <= t + k < n)


def tile_at(j, u, k):
    q = u + k
    return 2 * j + q, j + q // 2, q % 2


def vit_tower(nc, I, out, h1_dram):
    with ExitStack() as ctx:
        def sb(name, shape, dt=F32):
            return ctx.enter_context(nc.sbuf_tensor(name, shape, dt))

        def sem(name):
            return ctx.enter_context(nc.semaphore(name))

        ident = sb("ident", [128, 128])
        nident = sb("nident", [C, C])
        headmask = sb("headmask", [128, HC])
        lin_w = sb("lin_w", [128, KP, D])
        lin_f = sb("lin_f", [128, KP, D])
        ln1_w = sb("ln1_w", [128, KP])
        ln1_b = sb("ln1_b", [128, KP])
        ln1_b_rep = sb("ln1_b_rep", [128, KP, C])
        lin_bias = sb("lin_bias", [C, D])
        ln2_w = sb("ln2_w", [C, D])
        pos = sb("pos", [C, D])
        pos_add = sb("pos_add", [C, D])
        wq = sb("wq", [128, KD, D])
        wk = sb("wk", [128, KD, D])
        wv = sb("wv", [128, KD, D])
        wo = sb("wo", [128, KD, D])
        bq = sb("bq", [128, KD])
        bk = sb("bk", [128, KD])
        bv = sb("bv", [C, D])
        bo = sb("bo", [C, D])
        mask_f = sb("mask_f", [4, 2 * C + 2 * HB * C])
        mask_b = sb("mask_b", [4, 2 * C + 2 * HB * C], BF16)
        sum_lhs = sb("sum_lhs", [C + 4, C], BF16)
        eps = sb("eps", [128, 1])
        mhalf = sb("mhalf", [128, 1])
        wg = sb("wg", [128, KD, F])
        wu = sb("wu", [128, KD, F])
        wd = sb("wd", [128, KF, D])
        bg = sb("bg", [128, KF])
        bg_half = sb("bg_half", [128, KF])
        bu = sb("bu", [128, KF])
        bd = sb("bd", [128, D])
        wqf = sb("wqf", [RET, 2 * PH, D])
        keys = sb("keys", [RET, 2 * PH, NK])
        simw = sb("simw", [128, KD, 2 * PH * NK])
        down = sb("down", [128, KD, NE])
        up = sb("up", [128, NE // 128, D])

        w_lin = sem("w_lin")
        w_a = sem("w_a")
        w_b = sem("w_b")
        w_b2 = sem("w_b2")
        const_f = sem("const_f")
        const_c = sem("const_c")
        mask_ready = sem("mask_ready")
        mask_moved = sem("mask_moved")
        rep_ready = sem("rep_ready")
        bias_ready = sem("bias_ready")
        heads_ready = sem("heads_ready")
        fold_ready = sem("fold_ready")
        bias_ps = sem("bias_ps")
        pos_ready = sem("pos_ready")
        pos_zero = sem("pos_zero")
        phase_a_ready = sem("phase_a_ready")
        h1_stored = [sem("h1_stored0"), sem("h1_stored1")]

        with ExitStack() as ca:
            def sa(name, shape, dt=F32):
                return ca.enter_context(nc.sbuf_tensor(name, shape, dt))

            def pa(name, shape):
                return ca.enter_context(nc.psum_tensor(name, shape, F32))

            xin = sa("xin", [C, 2, PD])
            xn = sa("xn", [C, 2, PD])
            st1 = sa("st1", [C, 2, 12])
            st2 = sa("st2", [C, 2, 6])
            st3 = sa("st3", [C, 2, 6])
            mv1 = sa("mv1", [C, 2, 2])
            mv2 = sa("mv2", [C, 2, 2])
            mv3 = sa("mv3", [C, 2, 2])
            ve = sa("ve", [C, 3, 1])
            rstd = sa("rstd", [C, 3, 2])
            xT = sa("xT", [128, KP, C])
            y = sa("y", [C, D])
            yn = sa("yn", [C, D])
            yw = sa("yw", [C, D])
            h = sa("h", [C, 2, D])
            hb = sa("hb", [C, 2, D])
            hn = sa("hn", [C, D])
            hnT = sa("hnT", [128, KD, C])
            qT = sa("qT", [128, KD, C])
            kT = sa("kT", [128, KD, C])
            qTb = sa("qTb", [128, KD, C], BF16)
            kTb = sa("kTb", [128, KD, C], BF16)
            headmask_b = sa("headmask_b", [128, HC, C], BF16)
            q_exp = sa("q_exp", [128, KD, HC, C])
            k_exp = sa("k_exp", [128, KD, HC, C], BF16)
            v_aug = sa("v_aug", [C, 2, H, DK + 1])
            mx = sa("mx", [C, H])
            diag = sa("diag", [C + 4, H, C], BF16)
            pT = sa("pT", [C, H, C])
            rden = sa("rden", [C, H])
            o = sa("o", [C, D])
            oT = sa("oT", [128, KD, C])
            h1 = sa("h1", [C, 2, D])

            ps_x = pa("ps_x", [128, 512])
            ps_y = pa("ps_y", [128, 512])
            ps_l = pa("ps_l", [128, 512])
            ps_o = pa("ps_o", [128, 512])
            ps_s = pa("ps_s", [128, 4, 512])

            x_loaded = [ctx.enter_context(nc.semaphore(f"x_loaded{u}")) for u in (0, 1)]
            st1_ready = sem("st1_ready")
            mv1_ready = sem("mv1_ready")
            st2_ready = sem("st2_ready")
            mv2_ready = sem("mv2_ready")
            st3_ready = sem("st3_ready")
            mv3_ready = sem("mv3_ready")
            ve_ready = [ctx.enter_context(nc.semaphore(f"ve_ready{k}")) for k in range(3)]
            rstd1_ready = sem("rstd1_ready")
            rstd2_ready = sem("rstd2_ready")
            rstd3_ready = sem("rstd3_ready")
            xn_ready = sem("xn_ready")
            xT_ps = sem("xT_ps")
            xT_ready = sem("xT_ready")
            lin_ps = sem("lin_ps")
            y_ready = sem("y_ready")
            yn_ready = sem("yn_ready")
            yw_ready = sem("yw_ready")
            h_ready = sem("h_ready")
            hb_ready = sem("hb_ready")
            hn_ready = sem("hn_ready")
            hnT_ps = sem("hnT_ps")
            hnT_ready = sem("hnT_ready")
            k_ps = sem("k_ps")
            q_ps = sem("q_ps")
            kb_ready = sem("kb_ready")
            v_ps = sem("v_ps")
            qk_ready = sem("qk_ready")
            qb_ready = sem("qb_ready")
            kexp_ready = sem("kexp_ready")
            qexp_ready = sem("qexp_ready")
            v_ready = sem("v_ready")
            s_ps = sem("s_ps")
            max_ready = sem("max_ready")
            diag_ready = sem("diag_ready")
            st_ps = sem("st_ps")
            p_ready = sem("p_ready")
            pv_ps = sem("pv_ps")
            rden_ready = sem("rden_ready")
            o_ready = sem("o_ready")
            oT_ps = sem("oT_ps")
            oT_ready = sem("oT_ready")
            wo_ps = sem("wo_ps")
            h1_ready = sem("h1_ready")

            block = ca.enter_context(nc.Block())

            loads_lin = [
                (ln1_b[:, :], I["ln1_b"]), (ln1_w[:, :], I["ln1_w"]), (ident[:, :], I["ident"]),
                (lin_bias[:, :], I["lin_b"].to_broadcast([C, D])), (mask_f[:, :], I["mask"]),
            ]
            loads_a = [
                (headmask[:, :], I["headmask"]), (nident[:, :], I["nident"]),
                (bk[:, :], I["bk"]), (bq[:, :], I["bq"]),
                (bv[:, :], I["bv"].to_broadcast([C, D])), (wk[:, :, :], I["wk"]),
                (wq[:, :, :], I["wq"]), (bo[:, :], I["bo"].to_broadcast([C, D])),
            ]
            loads_a2 = [(wv[:, :, :], I["wv"]), (wo[:, :, :], I["wo"])]
            loads_rows = []
            for g in range(G):
                loads_rows += [
                    (ln2_w[g * S + 1:(g + 1) * S, :], I["ln2_w"].to_broadcast([NP_, D])),
                    (pos_add[g * S + 1:(g + 1) * S, :], I["ln2_b"].to_broadcast([NP_, D])),
                    (pos_add[g * S:g * S + 1, :], I["cls"]),
                    (pos[g * S:(g + 1) * S, :], I["pos"]),
                ]
            loads_b = [
                (wqf[:, :, :], I["wqf"]), (keys[:, :, :], I["keys"]), (down[:, :, :], I["down"]),
                (wg[:, :, :], I["wg"]), (wu[:, :, :], I["wu"]), (bg[:, :], I["bg"]), (bu[:, :], I["bu"]),
                (wd[:, :, :], I["wd"]), (up[:, :, :], I["up"]), (bd[:, :], I["bd"].to_broadcast([128, D])),
            ]
            n_loads_lin = 16 * (len(loads_lin) + 1)
            n_loads_a = 16 * (len(loads_a) + len(loads_a2))
            n_loads_rows = 16 * len(loads_rows)

            @block.sync
            def _(sp):
                def load_x(t, j, u):
                    if late(t, 2):
                        sp.wait_ge(xn_ready, t - 1)
                    sp.dma_start(xin[:, u, :], I["x"][t, :, :]).then_inc(x_loaded[u], 16)

                def store(t, j, u):
                    sp.wait_ge(h1_ready, t + 1)
                    if isinstance(t, int) and t == NA - 1:
                        new = B - (NA - 1) * G
                        sp.dma_start(h1_dram[(B - new) * S:B * S, :],
                                     h1[R - new * S:R, u, :]).then_inc(h1_stored[u], 16)
                    else:
                        sp.dma_start(h1_dram[bass.ds(t * R, R), :], h1[0:R, u, :]).then_inc(h1_stored[u], 16)

                def body(j, u, has):
                    if has(4) and late(tile_at(j, u, 4)[0], 4):
                        load_x(*tile_at(j, u, 4))
                    if has(-1):
                        store(*tile_at(j, u, -1))

                load_x(0, 0, 0)
                sp.dma_start(lin_w[:, :, :], I["lin_w"]).then_inc(w_lin, 16)
                load_x(1, 0, 1)
                for dst, src in loads_a2:
                    sp.dma_start(dst, src).then_inc(w_a, 16)
                sp.wait_ge(pos_zero, 3)
                for dst, src in loads_rows:
                    sp.dma_start(dst, src).then_inc(w_b, 16)
                load_x(2, 1, 0)
                load_x(3, 1, 1)
                sp.wait_ge(mask_ready, 1)
                for r in range(H // HB):
                    sp.dma_start(diag[C:C + 4, r * HB:(r + 1) * HB, :],
                                 mask_b[:, 2 * C + HB * C:2 * C + 2 * HB * C]
                                 .rearrange("p (a b) -> p a b", a=HB)).then_inc(mask_moved, 16)
                sp.wait_ge(const_c, 1)
                sp.dma_start(sum_lhs[C:C + 4, :], mask_b[:, C:2 * C]).then_inc(mask_moved, 16)
                for dst, src in loads_b:
                    sp.dma_start(dst, src).then_inc(w_b2, 16)
                steps(sp, body, NA, 4, 1)
                sp.wait_ge(w_b2, 16 * len(loads_b))
                for u in (0, 1):
                    sp.wait_ge(h1_stored[u], 16 * ((NA + 1 - u) // 2))

            @block.gpsimd
            def _(pool):
                pool.memset(ln2_w[:, :], 0.0).then_inc(pos_zero, 1)
                pool.memset(pos_add[:, :], 0.0).then_inc(pos_zero, 1)
                pool.memset(pos[:, :], 0.0).then_inc(pos_zero, 1)
                pool.memset(sum_lhs[:, :], 1.0).then_inc(const_c, 1)
                pool.memset(eps[:, :], EPS).then_inc(const_f, 1)
                pool.memset(mhalf[:, :], -0.5).then_inc(const_f, 1)
                pool.wait_ge(const_f, 2)

                def make_rstd(k, t, var, dst):
                    pool.tensor_tensor(ve[:, k, :], var, eps[0:C, :], ALU.add).then_inc(ve_ready[k], 1)
                    pool.wait_ge(ve_ready[k], t + 1)
                    return pool.tensor_tensor(dst, ve[:, k, :], mhalf[0:C, :], ALU.pow)

                def body(j, u, has):
                    if has(1):
                        t, _, u1 = tile_at(j, u, 1)
                        pool.wait_ge(mv2_ready, t + 1)
                        make_rstd(1, t, mv2[:, u1, 1:2], rstd[:, 1, u1:u1 + 1]).then_inc(rstd2_ready, 1)
                    if has(0):
                        t = tile_at(j, u, 0)[0]
                        for half in (0, 1):
                            heads = slice(half * H // 2, (half + 1) * H // 2)
                            pool.wait_ge(max_ready, 4 * t + 2 * half + 2)
                            pool.tensor_tensor(diag[0:C, heads, :],
                                               nident[:, :].unsqueeze(1).to_broadcast([C, H // 2, C]),
                                               mx[:, heads].unsqueeze(2).to_broadcast([C, H // 2, C]),
                                               ALU.mult).then_inc(diag_ready, 1)
                    if has(3):
                        t, _, u3 = tile_at(j, u, 3)
                        pool.wait_ge(mv1_ready, t + 1)
                        make_rstd(0, t, mv1[:, u3, 1:2], rstd[:, 0, u3:u3 + 1]).then_inc(rstd1_ready, 1)
                    if has(1):
                        t, _, u1 = tile_at(j, u, 1)
                        pool.wait_ge(mv3_ready, t + 1)
                        make_rstd(2, t, mv3[:, u1, 1:2], rstd[:, 2, u1:u1 + 1]).then_inc(rstd3_ready, 1)
                    if has(1):
                        t, _, u1 = tile_at(j, u, 1)
                        if not late(t, 1):
                            pool.wait_ge(w_a, n_loads_a)
                        pool.wait_ge(h_ready, t + 1)
                        if late(t, 2):
                            pool.wait_ge(h1_ready, t - 1)
                        pool.tensor_tensor(hb[:, u1, :], h[:, u1, :], bo[:, :], ALU.add).then_inc(hb_ready, 1)

                steps(pool, body, NA, 3, 1)

            @block.vector
            def _(dve):
                dve.memset(v_aug[:, :, :, :], 1.0).then_inc(heads_ready, 1)

                def masks():
                    dve.wait_ge(w_lin, n_loads_lin)
                    dve.tensor_copy(ln1_b_rep[:, :, :],
                                    ln1_b[:, :].unsqueeze(2).to_broadcast([128, KP, C])).then_inc(rep_ready, 1)
                    dve.tensor_copy(mask_b[:, :], mask_f[:, :]).then_inc(mask_ready, 1)

                def fold_gain():
                    dve.tensor_tensor(lin_f[:, :, :], lin_w[:, :, :],
                                      ln1_w[:, :].unsqueeze(2).to_broadcast([128, KP, D]),
                                      ALU.mult).then_inc(fold_ready, 1)

                def fold_bias():
                    dve.wait_ge(bias_ps, 1)
                    dve.tensor_tensor(lin_bias[:, :], ps_o[0:C, 0:D], lin_bias[:, :], ALU.add).then_inc(bias_ready, 1)
                    dve.wait_ge(bias_ready, 1)

                def positions():
                    dve.wait_ge(w_b, n_loads_rows)
                    dve.tensor_tensor(pos_add[:, :], pos_add[:, :], pos[:, :], ALU.add).then_inc(pos_ready, 1)
                    dve.wait_ge(pos_ready, 1)

                def head_masks():
                    dve.wait_ge(w_a, n_loads_a)
                    dve.tensor_copy(headmask_b[:, :, :],
                                    headmask[:, :].unsqueeze(2).to_broadcast([128, HC, C])).then_inc(heads_ready, 1)
                    dve.wait_ge(heads_ready, 2)

                def aggregate(ready, mv, st, done, t, u):
                    if isinstance(t, int):
                        dve.wait_ge(ready, t + 1)
                    dve.bn_aggr(mv[:, u, :], st[:, u, :]).then_inc(done, 1)

                def normaliser(t, j, u):
                    if not isinstance(t, int):
                        dve.wait_ge(st2_ready, t + 3)
                    dve.wait_ge(pv_ps, t + 1)
                    pv = ps_o[0:C, 0:H * (DK + 1)].rearrange("p (h d) -> p h d", h=H)
                    dve.reciprocal(rden[:, :], pv[:, :, DK]).then_inc(rden_ready, 1)

                def normalise(t, j, u):
                    dve.wait_ge(rden_ready, t + 1)
                    pv = ps_o[0:C, 0:H * (DK + 1)].rearrange("p (h d) -> p h d", h=H)
                    dve.tensor_tensor(o[:, :].rearrange("p (h d) -> p h d", h=H), pv[:, :, 0:DK],
                                      rden[:, :].unsqueeze(2).to_broadcast([C, H, DK]),
                                      ALU.mult).then_inc(o_ready, 1)

                def row_max(t, j, u):
                    for b in range(4):
                        dve.wait_ge(s_ps, 4 * t + b + 1)
                        dve.tensor_reduce(mx[:, b * HB:(b + 1) * HB],
                                          ps_s[0:C, b, 0:HB * C].rearrange("p (h k) -> p h k", h=HB),
                                          AX, ALU.max).then_inc(max_ready, 1)

                def residual(t, j, u):
                    dve.wait_ge(wo_ps, t + 1)
                    dve.wait_ge(hb_ready, t + 1)
                    if late(t, 2):
                        dve.wait_ge(h1_stored[u], 16 * j)
                    if not isinstance(t, int):
                        dve.wait_ge(st3_ready, t + 3)
                    dve.tensor_tensor(h1[:, u, :], ps_o[0:C, 0:D], hb[:, u, :], ALU.add).then_inc(h1_ready, 1)

                def stats1(t, j, u):
                    dve.wait_ge(x_loaded[u], 16 * (j + 1))
                    dve.bn_stats(st1[:, u, 0:6], xin[:, u, 0:PD // 2])
                    dve.bn_stats(st1[:, u, 6:12], xin[:, u, PD // 2:PD]).then_inc(st1_ready, 1)

                def norm1(t, j, u):
                    if not late(t, 1):
                        masks()
                    dve.wait_ge(rstd1_ready, t + 1)
                    if late(t, 2):
                        dve.wait_ge(xT_ps, t - 1)
                    dve.tensor_scalar(xn[:, u, :], xin[:, u, :], mv1[:, u, 0:1], rstd[:, 0, u:u + 1],
                                      ALU.subtract, ALU.mult).then_inc(xn_ready, 1)
                    if not late(t, 1):
                        fold_gain()

                def embed(t, j, u):
                    if not late(t, 1):
                        fold_bias()
                    dve.wait_ge(lin_ps, t + 1)
                    dve.tensor_tensor(y[:, :], ps_l[0:C, 0:D], lin_bias[:, :], ALU.add).then_inc(y_ready, 1)
                    dve.wait_ge(y_ready, t + 1)
                    dve.bn_stats(st2[:, u, :], y[:, :]).then_inc(st2_ready, 1)

                def layer_norm2(t, j, u):
                    dve.wait_ge(rstd2_ready, t + 1)
                    dve.tensor_scalar(yn[:, :], y[:, :], mv2[:, u, 0:1], rstd[:, 1, u:u + 1],
                                      ALU.subtract, ALU.mult).then_inc(yn_ready, 1)

                def weigh(t, j, u):
                    if not late(t, 1):
                        positions()
                    if not isinstance(t, int):
                        dve.wait_ge(st1_ready, t + 3)
                    dve.wait_ge(yn_ready, t + 1)
                    dve.tensor_tensor(yw[:, :], yn[:, :], ln2_w[:, :], ALU.mult).then_inc(yw_ready, 1)

                def tokens(t, j, u):
                    dve.wait_ge(yw_ready, t + 1)
                    dve.tensor_tensor(h[:, u, :], yw[:, :], pos_add[:, :], ALU.add).then_inc(h_ready, 1)
                    dve.wait_ge(h_ready, t + 1)
                    dve.bn_stats(st3[:, u, :], h[:, u, :]).then_inc(st3_ready, 1)

                def norm3(t, j, u):
                    dve.wait_ge(rstd3_ready, t + 1)
                    dve.tensor_scalar(hn[:, :], h[:, u, :], mv3[:, u, 0:1], rstd[:, 2, u:u + 1],
                                      ALU.subtract, ALU.mult).then_inc(hn_ready, 1)

                def copy_hnT(t, j, u):
                    dve.wait_ge(hnT_ps, t + 1)
                    dve.tensor_copy(hnT[:, :, :],
                                    ps_y[:, 0:KD * C].rearrange("p (k c) -> p k c", k=KD)).then_inc(hnT_ready, 1)

                def expand(t, j, u):
                    if not late(t, 1):
                        head_masks()
                    dve.wait_ge(v_ps, t + 1)
                    dve.tensor_tensor(v_aug[:, u, :, 0:DK],
                                      ps_o[0:C, 0:D].rearrange("p (h d) -> p h d", h=H),
                                      bv[:, :].rearrange("p (h d) -> p h d", h=H), ALU.add).then_inc(v_ready, 1)
                    dve.wait_ge(kb_ready, t + 1)
                    for c in range(KD):
                        i = dve.tensor_tensor(k_exp[:, c, :, :], kTb[:, c, :].unsqueeze(1).to_broadcast([128, HC, C]),
                                              headmask_b[:, :, :], ALU.mult)
                    i.then_inc(kexp_ready, 1)
                    dve.wait_ge(qk_ready, t + 1)
                    for c in range(KD):
                        i = dve.tensor_tensor(q_exp[:, c, :, :], qT[:, c, :].unsqueeze(1).to_broadcast([128, HC, C]),
                                              headmask[:, :].unsqueeze(2).to_broadcast([128, HC, C]), ALU.mult)
                    i.then_inc(qexp_ready, 1)

                def body(j, u, has):
                    t1, u1 = tile_at(j, u, 1)[::2]
                    t3, u3 = tile_at(j, u, 3)[::2]
                    if has(1):
                        embed(*tile_at(j, u, 1))
                    if has(-1):
                        normaliser(*tile_at(j, u, -1))
                    if has(1):
                        aggregate(st2_ready, mv2, st2, mv2_ready, t1, u1)
                    if has(-1):
                        normalise(*tile_at(j, u, -1))
                    if has(0):
                        row_max(*tile_at(j, u, 0))
                    if has(1):
                        layer_norm2(*tile_at(j, u, 1))
                    if has(3):
                        stats1(*tile_at(j, u, 3))
                    if has(1):
                        weigh(*tile_at(j, u, 1))
                    if has(3):
                        aggregate(st1_ready, mv1, st1, mv1_ready, t3, u3)
                    if has(1):
                        tokens(*tile_at(j, u, 1))
                    if has(-1):
                        residual(*tile_at(j, u, -1))
                    if has(1):
                        aggregate(st3_ready, mv3, st3, mv3_ready, t1, u1)
                    if has(3):
                        norm1(*tile_at(j, u, 3))
                    if has(1):
                        norm3(*tile_at(j, u, 1))
                        copy_hnT(*tile_at(j, u, 1))
                        expand(*tile_at(j, u, 1))

                steps(dve, body, NA, 3, 1)

            @block.scalar
            def _(act):
                def copy_xT(t, j, u):
                    act.wait_ge(xT_ps, t + 1)
                    if late(t, 1):
                        act.wait_ge(lin_ps, t)
                    act.activation(xT[:, 0:4, :], ps_x[:, 0:4 * C].rearrange("p (k c) -> p k c", k=4), ACT.Copy)
                    act.activation(xT[:, 4:KP, :], ps_y[:, 0:2 * C].rearrange("p (k c) -> p k c", k=2),
                                   ACT.Copy).then_inc(xT_ready, 1)

                def copy_oT(t, j, u):
                    act.wait_ge(oT_ps, t + 1)
                    act.activation(oT[:, :, :], ps_o[:, 0:KD * C].rearrange("p (k c) -> p k c", k=KD),
                                   ACT.Copy).then_inc(oT_ready, 1)

                def exp_scores(t, j, u):
                    for b in range(4):
                        act.wait_ge(st_ps, 4 * t + b + 1)
                        i = act.activation(pT[:, b * HB:(b + 1) * HB, :],
                                           ps_s[0:C, b, 0:HB * C].rearrange("p (h q) -> p h q", h=HB),
                                           ACT.Exp, scale=float(DK) ** -0.5)
                    i.then_inc(p_ready, 1)

                def copy_qk(t, j, u):
                    if not late(t, 1):
                        act.wait_ge(w_a, n_loads_a)
                    act.wait_ge(k_ps, t + 1)
                    if late(t, 1):
                        act.wait_ge(qexp_ready, t)
                    for c in range(KD):
                        i = act.activation(kTb[:, c, :], ps_x[:, c * C:(c + 1) * C], ACT.Identity,
                                           bias=bk[:, c:c + 1])
                    i.then_inc(kb_ready, 1)
                    for c in range(KD):
                        act.activation(kT[:, c, :], ps_x[:, c * C:(c + 1) * C], ACT.Identity,
                                       bias=bk[:, c:c + 1])
                    act.wait_ge(q_ps, t + 1)
                    for c in range(KD):
                        i = act.activation(qT[:, c, :], ps_y[:, c * C:(c + 1) * C], ACT.Identity,
                                           bias=bq[:, c:c + 1])
                    i.then_inc(qk_ready, 1)
                    act.wait_ge(qk_ready, t + 1)
                    act.activation(qTb[:, :, :], qT[:, :, :], ACT.Copy).then_inc(qb_ready, 1)

                def body(j, u, has):
                    if has(-1):
                        copy_oT(*tile_at(j, u, -1))
                    if has(2):
                        copy_xT(*tile_at(j, u, 2))
                    if has(0):
                        exp_scores(*tile_at(j, u, 0))
                    if has(1):
                        copy_qk(*tile_at(j, u, 1))

                for dst, src in loads_lin:
                    act.dma_start(dst, src).then_inc(w_lin, 16)
                for dst, src in loads_a:
                    act.dma_start(dst, src).then_inc(w_a, 16)
                steps(act, body, NA, 3, 1)

            @block.tensor
            def _(pe):
                pe.wait_ge(w_lin, n_loads_lin)
                pe.wait_ge(rep_ready, 1)
                for k in range(KP):
                    i = pe.matmul(ps_o[0:C, 0:D], ln1_b_rep[:, k, :], lin_w[:, k, :], start=k == 0, stop=k == KP - 1)
                i.then_inc(bias_ps, 1)

                def transpose_x(t, j, u):
                    pe.wait_ge(xn_ready, t + 1)
                    if late(t, 2):
                        pe.wait_ge(qk_ready, t - 1)
                    for k in range(KP):
                        dst = ps_x[:, k * C:(k + 1) * C] if k < 4 else ps_y[:, (k - 4) * C:(k - 3) * C]
                        i = pe.transpose(dst, xn[:, u, k * 128:(k + 1) * 128], ident[0:C, 0:C])
                    i.then_inc(xT_ps, 1)

                def transpose_o(t, j, u):
                    pe.wait_ge(o_ready, t + 1)
                    for k in range(KD):
                        i = pe.transpose(ps_o[:, k * C:(k + 1) * C], o[:, k * 128:(k + 1) * 128], ident[0:C, 0:C])
                    i.then_inc(oT_ps, 1)

                def scores_for_max(t, j, u):
                    if not late(t, 1):
                        pe.wait_ge(mask_moved, 16 * (H // HB + 1))
                    pe.wait_ge(kexp_ready, t + 1)
                    pe.wait_ge(qb_ready, t + 1)
                    if late(t, 1):
                        pe.wait_ge(p_ready, t)
                    for b in range(4):
                        c, s0 = b // 2, (b % 2) * HB
                        pe.matmul(ps_s[0:C, b, 0:HB * C], qTb[:, c, :], k_exp[:, c, s0:s0 + HB, :],
                                  start=True, stop=False)
                        pe.matmul(ps_s[0:C, b, 0:HB * C], mask_b[:, 0:C], mask_b[:, 2 * C:2 * C + HB * C],
                                  start=False, stop=True).then_inc(s_ps, 1)

                def project_o(t, j, u):
                    pe.wait_ge(oT_ready, t + 1)
                    for k in range(KD):
                        i = pe.matmul(ps_o[0:C, 0:D], oT[:, k, :], wo[:, k, :], start=k == 0, stop=k == KD - 1)
                    i.then_inc(wo_ps, 1)

                def scores(t, j, u):
                    pe.wait_ge(qexp_ready, t + 1)
                    for b in range(4):
                        c, s0 = b // 2, (b % 2) * HB
                        pe.wait_ge(max_ready, 4 * t + b + 1)
                        pe.matmul(ps_s[0:C, b, 0:HB * C], kT[:, c, :], q_exp[:, c, s0:s0 + HB, :],
                                  start=True, stop=False)

                def transpose_hn(t, j, u, has_next):
                    if has_next:
                        pe.wait_ge(xT_ready, t + 2)
                    pe.wait_ge(hn_ready, t + 1)
                    for k in range(KD):
                        i = pe.transpose(ps_y[:, k * C:(k + 1) * C], hn[:, k * 128:(k + 1) * 128], ident[0:C, 0:C])
                    i.then_inc(hnT_ps, 1)

                def shift(t, j, u):
                    for b in range(4):
                        if b % 2 == 0:
                            pe.wait_ge(diag_ready, 2 * t + b // 2 + 1)
                        pe.matmul(ps_s[0:C, b, 0:HB * C], sum_lhs[:, :], diag[:, b * HB:(b + 1) * HB, :],
                                  start=False, stop=True).then_inc(st_ps, 1)

                def project_v(t, j, u):
                    pe.wait_ge(hnT_ready, t + 1)
                    if not late(t, 1):
                        pe.wait_ge(w_a, n_loads_a)
                        pe.wait_ge(bias_ready, 1)
                    if late(t, 2):
                        pe.wait_ge(h1_ready, t - 1)
                    for k in range(KD):
                        i = pe.matmul(ps_o[0:C, 0:D], hnT[:, k, :], wv[:, k, :], start=k == 0, stop=k == KD - 1)
                    i.then_inc(v_ps, 1)

                def project(w, ps, m, done):
                    for k in range(KD):
                        i = pe.matmul(ps[:, m * C:(m + 1) * C], w[:, k, m * 128:(m + 1) * 128], hnT[:, k, :],
                                      start=k == 0, stop=k == KD - 1)
                    if m == KD - 1:
                        i.then_inc(done, 1)

                def linear(t, k):
                    if k == 0:
                        pe.wait_ge(xT_ready, t + 1)
                        if late(t, 1):
                            pe.wait_ge(y_ready, t)
                        else:
                            pe.wait_ge(fold_ready, 1)
                    i = pe.matmul(ps_l[0:C, 0:D], xT[:, k, :], lin_f[:, k, :], start=k == 0, stop=k == KP - 1)
                    if k == KP - 1:
                        i.then_inc(lin_ps, 1)

                def weighted_values(t, u, n, has_next):
                    if n == 0:
                        pe.wait_ge(p_ready, t + 1)
                        if has_next:
                            pe.wait_ge(v_ready, t + 2)
                        else:
                            pe.wait_ge(v_ready, t + 1)
                            pe.wait_ge(h1_ready, t)
                    i = pe.matmul(ps_o[0:C, n * (DK + 1):(n + 1) * (DK + 1)], pT[:, n, :],
                                  v_aug[:, u, n, :], start=True, stop=True)
                    if n == H - 1:
                        i.then_inc(pv_ps, 1)

                def body(j, u, has):
                    if has(0):
                        scores_for_max(*tile_at(j, u, 0))
                    if has(-1):
                        transpose_o(*tile_at(j, u, -1))
                    if has(2):
                        transpose_x(*tile_at(j, u, 2))
                    if has(-1):
                        project_o(*tile_at(j, u, -1))
                    if has(0):
                        scores(*tile_at(j, u, 0))
                        shift(*tile_at(j, u, 0))
                    t0, t2 = tile_at(j, u, 0)[0], tile_at(j, u, 2)[0]
                    if has(2):
                        for k in (0, 1):
                            linear(t2, k)
                    if has(1):
                        transpose_hn(*tile_at(j, u, 1), has(2))
                    if has(1):
                        project_v(*tile_at(j, u, 1))
                        for m in range(KD):
                            project(wk, ps_x, m, k_ps)
                    for k in range(2, KP):
                        if has(1) and k < 2 + KD:
                            project(wq, ps_y, k - 2, q_ps)
                        if has(2):
                            linear(t2, k)
                        if has(0):
                            for n in range((k - 2) * H // (KP - 2), (k - 1) * H // (KP - 2)):
                                weighted_values(t0, u, n, has(1))

                steps(pe, body, NA, 3, 1)
        with ExitStack() as cb:
            def sbb(name, shape, dt=F32):
                return cb.enter_context(nc.sbuf_tensor(name, shape, dt))

            def pb(name, shape):
                return cb.enter_context(nc.psum_tensor(name, shape, F32))

            hx = sbb("hx", [128, 4, D])
            hxb = sbb("hxb", [128, 2, D])
            stf = sbb("stf", [128, 2, 6])
            mvf = sbb("mvf", [128, 2, 2])
            vef = sbb("vef", [128, 1])
            rstdf = sbb("rstdf", [128, 2])
            hf = sbb("hf", [128, D])
            hfT = sbb("hfT", [128, KD, 128])
            sims = sbb("sims", [128, 2, 2, PH, NK])
            gate = sbb("gate", [128, 2, KF, 128])
            gate_t = sbb("gate_t", [128, 2, KF, 128])
            upp = sbb("upp", [128, 2, KF, 128])
            act_a = sbb("act_a", [128, KF, 128])
            hid = sbb("hid", [128, KF, 128])
            de_t = sbb("de_t", [128, NE])
            silu2 = sbb("silu2", [128, NE])
            top = sbb("top", [128, 2, PH, T8])
            grid = sbb("grid", [128, PH, T8, T8])
            best = sbb("best", [128, PH, T8])
            rel = sbb("rel", [128, PH, T8])
            erel = sbb("erel", [128, PH, T8])
            neg_m = sbb("neg_m", [128, PH])
            zsum = sbb("zsum", [128, PH])
            rz = sbb("rz", [128, PH])
            pair = sbb("pair", [128, PH, XR, NK])
            epair = sbb("epair", [128, PH, XR, NK])
            picked = sbb("picked", [128, PH])
            rest = sbb("rest", [128, PH])
            restw = sbb("restw", [128, PH])
            rest1 = sbb("rest1", [128, 1])
            coef = sbb("coef", [128, 2, NE])
            wgt = sbb("wgt", [128, NE])
            wT = sbb("wT", [128, NE // 128, 128])
            res = sbb("res", [128, 2, D])

            ps_m = pb("ps_m", [128, 512])
            ps_out = pb("ps_out", [128, 512])
            ps_e = pb("ps_e", [128, 2, 512])
            ps_g = pb("ps_g", [128, 2, 512])
            ps_u = pb("ps_u", [128, 2, 512])

            names = ("w_loaded w2_ready simw_ps simw_ready h_loaded0 h_loaded1 h_loaded2 h_loaded3 "
                     "stf_ready mvf_ready vef_ready rstdf_ready hf_ready hxb_ready hfT_ps hfT_ready "
                     "sim_ps sims_ready e_ps e_tanh gate_ps up_ps gate_ready gate_t_ready up_ready "
                     "silu_ready top_ready grid_ready best_ready rel_ready negm_ready erel_ready z_ready "
                     "rz_ready pair_ready epair_ready picked_ready act_ready hid_ready coef_step "
                     "rest_ready restw_ready rest1_ready coef_ready wgt_ready wT_ps wT_ready out_ps "
                     "res_ready stored0 stored1").split()
            q = {n: cb.enter_context(nc.semaphore("b_" + n)) for n in names}
            stored = [q["stored0"], q["stored1"]]
            h_loaded = [q[f"h_loaded{i}"] for i in range(4)]
            block = cb.enter_context(nc.Block())

            def rows_at(t):
                return N - 128 if isinstance(t, int) and t == NB - 1 else t * 128

            @block.sync
            def _(sp):
                def load_h(t, j, u):
                    if late(t, 2):
                        sp.wait_ge(q["hf_ready"], t - 1)
                        sp.wait_ge(q["hxb_ready"], t - 1)
                    sp.dma_start(hx[:, u, :], h1_dram[bass.ds(rows_at(t), 128), :]).then_inc(h_loaded[u], 16)

                def store(t, j, u):
                    sp.wait_ge(q["res_ready"], t + 1)
                    new = N - (NB - 1) * 128 if isinstance(t, int) and t == NB - 1 else 128
                    sp.dma_start(out[bass.ds(rows_at(t) + 128 - new, new), :],
                                 res[128 - new:128, u, :]).then_inc(stored[u], 16)

                def body(j, u, has):
                    if has(2):
                        load_h(*tile_at(j, u, 2))
                    if has(-1):
                        store(*tile_at(j, u, -1))

                steps(sp, body, NB, 2, 1)
                for u in (0, 1):
                    sp.wait_ge(stored[u], 16 * ((NB + 1 - u) // 2))

            @block.gpsimd
            def _(pool):
                def body(j, u, has):
                    if has(1):
                        t, tj, tu = tile_at(j, u, 1)
                        pool.wait_ge(q["mvf_ready"], t + 1)
                        pool.tensor_tensor(vef[:, :], mvf[:, tu, 1:2], eps[:, :], ALU.add).then_inc(q["vef_ready"], 1)
                        pool.wait_ge(q["vef_ready"], t + 1)
                        pool.tensor_tensor(rstdf[:, tu:tu + 1], vef[:, :], mhalf[:, :],
                                           ALU.pow).then_inc(q["rstdf_ready"], 1)
                        if late(t, 2):
                            pool.wait_ge(q["res_ready"], t - 1)
                        pool.tensor_tensor(hxb[:, tu, :], hx[:, tu, :], bd[:, :], ALU.add).then_inc(q["hxb_ready"], 1)

                steps(pool, body, NB, 2, 1)

            @block.vector
            def _(dve):
                dve.tensor_scalar(bg_half[:, :], bg[:, :], 0.5, None, ALU.mult).then_inc(q["w2_ready"], 1)
                dve.wait_ge(q["simw_ps"], 1)
                dve.tensor_copy(simw[:, :, :], ps_g[:, :, :]).then_inc(q["simw_ready"], 1)

                def stats(t, j, u):
                    dve.wait_ge(h_loaded[u], 16 * (j + 1))
                    dve.bn_stats(stf[:, u, :], hx[:, u, :]).then_inc(q["stf_ready"], 1)

                def aggregate(t, j, u):
                    if isinstance(t, int):
                        dve.wait_ge(q["stf_ready"], t + 1)
                    dve.bn_aggr(mvf[:, u, :], stf[:, u, :]).then_inc(q["mvf_ready"], 1)

                def norm(t, j, u):
                    dve.wait_ge(q["rstdf_ready"], t + 1)
                    if late(t, 1):
                        dve.wait_ge(q["hfT_ps"], t)
                    dve.tensor_scalar(hf[:, :], hx[:, u, :], mvf[:, u, 0:1], rstdf[:, u:u + 1],
                                      ALU.subtract, ALU.mult).then_inc(q["hf_ready"], 1)

                def expert_silu(t, j, u):
                    if not isinstance(t, int):
                        dve.wait_ge(q["stf_ready"], t + 2)
                    dve.wait_ge(q["sims_ready"], t + 1)
                    if late(t, 1):
                        dve.wait_ge(q["wgt_ready"], t)
                    dve.wait_ge(q["e_tanh"], t + 1)
                    dve.scalar_tensor_tensor(silu2[:, :], de_t[:, :], 1.0, ps_e[:, :, :].rearrange("p a b -> p (a b)"),
                                             ALU.add, ALU.mult).then_inc(q["silu_ready"], 1)

                def top_keys(t, j, u):
                    for p in range(2):
                        for n in range(PH):
                            i = dve.max(top[:, p, n, :], sims[:, u, p, n, :])
                    i.then_inc(q["top_ready"], 1)

                def top_pairs(t, j, u):
                    dve.wait_ge(q["top_ready"], t + 1)
                    dve.tensor_tensor(grid[:, :, :, :],
                                      top[:, 0, :, :].unsqueeze(3).to_broadcast([128, PH, T8, T8]),
                                      top[:, 1, :, :].unsqueeze(2).to_broadcast([128, PH, T8, T8]),
                                      ALU.add).then_inc(q["grid_ready"], 1)

                def best_pairs(t, j, u):
                    for n in range(PH):
                        i = dve.max(best[:, n, :], grid[:, n, :, :].rearrange("p a b -> p (a b)"))
                    i.then_inc(q["best_ready"], 1)

                def relative(t, j, u):
                    dve.wait_ge(q["best_ready"], t + 1)
                    dve.tensor_scalar(neg_m[:, :], best[:, :, 0], -1.0, None, ALU.mult).then_inc(q["negm_ready"], 1)
                    dve.tensor_tensor(rel[:, :, :], best[:, :, :],
                                      best[:, :, 0:1].to_broadcast([128, PH, T8]),
                                      ALU.subtract).then_inc(q["rel_ready"], 1)

                def normaliser(t, j, u):
                    dve.wait_ge(q["erel_ready"], t + 1)
                    dve.tensor_reduce(zsum[:, :], erel[:, :, :], AX, ALU.add).then_inc(q["z_ready"], 1)
                    dve.wait_ge(q["z_ready"], t + 1)
                    dve.reciprocal(rz[:, :], zsum[:, :]).then_inc(q["rz_ready"], 1)

                def pair_sums(t, j, u, n):
                    if n == 2:
                        dve.wait_ge(q["grid_ready"], t + 1)
                    dve.tensor_tensor(pair[:, n, :, :],
                                      sims[:, u, 0, n, 0:XR].unsqueeze(2).to_broadcast([128, XR, NK]),
                                      sims[:, u, 1, n, :].unsqueeze(1).to_broadcast([128, XR, NK]),
                                      ALU.add).then_inc(q["pair_ready"], 1)

                def pick(t, j, u, n):
                    dve.wait_ge(q["epair_ready"], PH * t + n + 1)
                    dve.scalar_tensor_tensor(pair[:, n, :, :].rearrange("p a b -> p (a b)"),
                                             pair[:, n, :, :].rearrange("p a b -> p (a b)"), best[:, n, T8 - 1:T8],
                                             epair[:, n, :, :].rearrange("p a b -> p (a b)"),
                                             ALU.is_ge, ALU.mult, accum_out=picked[:, n:n + 1]).then_inc(q["picked_ready"], 1)

                def combine(t, j, u, n):
                    dve.wait_ge(q["picked_ready"], PH * t + n + 1)
                    flat = pair[:, n, :, :].rearrange("p a b -> p (a b)")
                    if n == 0:
                        dve.wait_ge(q["rz_ready"], t + 1)
                        dve.tensor_scalar(coef[:, 0, :], flat, rz[:, 0:1], None, ALU.mult).then_inc(q["coef_step"], 1)
                    else:
                        dve.wait_ge(q["coef_step"], PH * t + n)
                        dve.scalar_tensor_tensor(coef[:, n % 2, :], flat, rz[:, n:n + 1], coef[:, 1 - n % 2, :],
                                                 ALU.mult, ALU.add).then_inc(q["coef_step"], 1)

                def rest_of(t, j, u):
                    dve.wait_ge(q["picked_ready"], PH * t + PH)
                    dve.tensor_tensor(rest[:, :], zsum[:, :], picked[:, :], ALU.subtract).then_inc(q["rest_ready"], 1)
                    dve.wait_ge(q["rest_ready"], t + 1)
                    dve.tensor_tensor(restw[:, :], rest[:, :], rz[:, :], ALU.mult).then_inc(q["restw_ready"], 1)
                    dve.wait_ge(q["restw_ready"], t + 1)
                    dve.tensor_reduce(rest1[:, :], restw[:, :], AX, ALU.add).then_inc(q["rest1_ready"], 1)

                def weights(t, j, u):
                    last = (PH - 1) % 2
                    dve.wait_ge(q["rest1_ready"], t + 1)
                    dve.wait_ge(q["coef_step"], PH * (t + 1))
                    dve.tensor_tensor(coef[:, last, NE - 1:NE], coef[:, last, NE - 1:NE], rest1[:, :],
                                      ALU.add).then_inc(q["coef_ready"], 1)
                    dve.wait_ge(q["coef_ready"], t + 1)
                    dve.scalar_tensor_tensor(wgt[:, :], silu2[:, :], 0.5, coef[:, last, :],
                                             ALU.mult, ALU.mult).then_inc(q["wgt_ready"], 1)

                def mlp_a(t, j, u):
                    dve.wait_ge(q["gate_t_ready"], t + 1)
                    dve.scalar_tensor_tensor(act_a[:, :, :], gate_t[:, u, :, :], 1.0, gate[:, u, :, :],
                                             ALU.add, ALU.mult).then_inc(q["act_ready"], 1)

                def mlp_b(t, j, u):
                    dve.wait_ge(q["act_ready"], t + 1)
                    dve.wait_ge(q["up_ready"], t + 1)
                    if late(t, 1):
                        dve.wait_ge(q["out_ps"], t)
                    dve.scalar_tensor_tensor(hid[:, :, :], act_a[:, :, :], 0.5, upp[:, u, :, :],
                                             ALU.mult, ALU.mult).then_inc(q["hid_ready"], 1)

                def result(t, j, u):
                    dve.wait_ge(q["hxb_ready"], t + 1)
                    dve.wait_ge(q["out_ps"], t + 1)
                    if late(t, 2):
                        dve.wait_ge(stored[u], 16 * j)
                    dve.tensor_tensor(res[:, u, :], ps_out[:, 0:D], hxb[:, u, :], ALU.add).then_inc(q["res_ready"], 1)

                def body(j, u, has):
                    now, nxt, prv = tile_at(j, u, 0), tile_at(j, u, 1), tile_at(j, u, -1)
                    if has(1):
                        stats(*nxt)
                    if has(0):
                        expert_silu(*now)
                    if has(1):
                        aggregate(*nxt)
                    if has(0):
                        top_keys(*now)
                    if has(1):
                        norm(*nxt)
                    if has(0):
                        pair_sums(*now, 0)
                        top_pairs(*now)
                        pair_sums(*now, 1)
                        pair_sums(*now, 2)
                        best_pairs(*now)
                        relative(*now)
                        pair_sums(*now, 3)
                        mlp_a(*now)
                    if has(-1):
                        result(*prv)
                    if has(0):
                        mlp_b(*now)
                        normaliser(*now)
                        pick(*now, 0)
                        pick(*now, 1)
                        combine(*now, 0)
                        pick(*now, 2)
                        combine(*now, 1)
                        pick(*now, 3)
                        combine(*now, 2)
                        rest_of(*now)
                        combine(*now, 3)
                        weights(*now)

                steps(dve, body, NB, 2, 1)

            @block.scalar
            def _(act):
                act.wait_ge(q["w2_ready"], 1)

                def front(t, j, u):
                    act.wait_ge(q["hfT_ps"], t + 1)
                    act.activation(hfT[:, :, :], ps_m[:, 0:D].rearrange("p (k c) -> p k c", k=KD),
                                   ACT.Copy).then_inc(q["hfT_ready"], 1)
                    act.wait_ge(q["sim_ps"], t + 1)
                    act.activation(sims[:, u, :, :, :].rearrange("p a b c -> p (a b c)"), ps_m[:, :],
                                   ACT.Copy).then_inc(q["sims_ready"], 1)

                def gate_up(t, j, u):
                    act.wait_ge(q["gate_ps"], t + 1)
                    for m in range(KF):
                        i = act.activation(gate[:, u, m, :], ps_g[:, m // 4, (m % 4) * 128:(m % 4 + 1) * 128],
                                           ACT.Identity, bias=bg[:, m:m + 1])
                    i.then_inc(q["gate_ready"], 1)
                    act.wait_ge(q["up_ps"], t + 1)
                    for m in range(KF):
                        i = act.activation(upp[:, u, m, :], ps_u[:, m // 4, (m % 4) * 128:(m % 4 + 1) * 128],
                                           ACT.Identity, bias=bu[:, m:m + 1])
                    i.then_inc(q["up_ready"], 1)
                    act.wait_ge(q["gate_ready"], t + 1)
                    act.activation(gate_t[:, u, :, :], gate[:, u, :, :], ACT.Tanh, scale=0.5).then_inc(q["gate_t_ready"], 1)

                def expert_tanh(t, j, u):
                    act.wait_ge(q["e_ps"], t + 1)
                    if late(t, 1):
                        act.wait_ge(q["silu_ready"], t)
                    act.activation(de_t[:, :], ps_e[:, :, :].rearrange("p a b -> p (a b)"), ACT.Tanh,
                                   scale=0.5).then_inc(q["e_tanh"], 1)

                def exps(t, j, u):
                    act.wait_ge(q["rel_ready"], t + 1)
                    act.activation(erel[:, :, :], rel[:, :, :], ACT.Exp).then_inc(q["erel_ready"], 1)
                    act.wait_ge(q["negm_ready"], t + 1)
                    for n in range(PH):
                        act.wait_ge(q["pair_ready"], PH * t + n + 1)
                        act.activation(epair[:, n, :, :], pair[:, n, :, :], ACT.Exp,
                                       bias=neg_m[:, n:n + 1]).then_inc(q["epair_ready"], 1)

                def copy_wT(t, j, u):
                    act.wait_ge(q["wT_ps"], t + 1)
                    if late(t, 1):
                        act.wait_ge(q["out_ps"], t)
                    act.activation(wT[:, :, :].rearrange("p a b -> p (a b)"),
                                   ps_g[:, :, :].rearrange("p a b -> p (a b)"), ACT.Copy).then_inc(q["wT_ready"], 1)

                def body(j, u, has):
                    now, nxt = tile_at(j, u, 0), tile_at(j, u, 1)
                    if has(1):
                        front(*nxt)
                    if has(0):
                        exps(*now)
                    if has(1):
                        expert_tanh(*nxt)
                        gate_up(*nxt)
                    if has(0):
                        copy_wT(*now)

                steps(act, body, NB, 2, 1)

            @block.tensor
            def _(pe):
                for k in range(KD):
                    for n in range(2 * PH):
                        i = pe.matmul(ps_g[:, k, n * NK:(n + 1) * NK], wqf[:, n, k * 128:(k + 1) * 128],
                                      keys[:, n, :], start=True, stop=True)
                i.then_inc(q["simw_ps"], 1)
                pe.wait_ge(q["simw_ready"], 1)

                def transpose_h(t, j, u):
                    pe.wait_ge(q["hf_ready"], t + 1)
                    if late(t, 1):
                        pe.wait_ge(q["sims_ready"], t)
                    for k in range(KD):
                        i = pe.transpose(ps_m[:, k * 128:(k + 1) * 128], hf[:, k * 128:(k + 1) * 128], ident[:, :])
                    i.then_inc(q["hfT_ps"], 1)

                def similarities(t, j, u):
                    pe.wait_ge(q["hfT_ready"], t + 1)
                    for k in range(KD):
                        i = pe.matmul(ps_m[:, :], hfT[:, k, :], simw[:, k, :], start=k == 0, stop=k == KD - 1)
                    i.then_inc(q["sim_ps"], 1)

                def experts(t, j, u):
                    if late(t, 1):
                        pe.wait_ge(q["silu_ready"], t)
                    for b in range(2):
                        for k in range(KD):
                            i = pe.matmul(ps_e[:, b, :], hfT[:, k, :], down[:, k, b * 512:(b + 1) * 512],
                                          start=k == 0, stop=k == KD - 1)
                    i.then_inc(q["e_ps"], 1)

                def gate_up(t, j, u):
                    if late(t, 2):
                        pe.wait_ge(q["wT_ready"], t - 1)
                    for ps, w, done in ((ps_g, wg, q["gate_ps"]), (ps_u, wu, q["up_ps"])):
                        if ps is ps_u and late(t, 1):
                            pe.wait_ge(q["up_ready"], t)
                        for m in range(KF):
                            for k in range(KD):
                                i = pe.matmul(ps[:, m // 4, (m % 4) * 128:(m % 4 + 1) * 128],
                                              w[:, k, m * 128:(m + 1) * 128], hfT[:, k, :],
                                              start=k == 0, stop=k == KD - 1)
                        i.then_inc(done, 1)

                def mlp_out(t, j, u):
                    pe.wait_ge(q["hid_ready"], t + 1)
                    if late(t, 1):
                        pe.wait_ge(q["res_ready"], t)
                    for m in range(KF):
                        pe.matmul(ps_out[:, 0:D], hid[:, m, :], wd[:, m, :], start=m == 0, stop=False)

                def transpose_w(t, j, u, has_next):
                    pe.wait_ge(q["wgt_ready"], t + 1)
                    if has_next:
                        pe.wait_ge(q["gate_ready"], t + 2)
                    for m in range(NE // 128):
                        i = pe.transpose(ps_g[:, m // 4, (m % 4) * 128:(m % 4 + 1) * 128],
                                         wgt[:, m * 128:(m + 1) * 128], ident[:, :])
                    i.then_inc(q["wT_ps"], 1)

                def experts_out(t, j, u):
                    pe.wait_ge(q["wT_ready"], t + 1)
                    for m in range(NE // 128):
                        i = pe.matmul(ps_out[:, 0:D], wT[:, m, :], up[:, m, :], start=False, stop=m == NE // 128 - 1)
                    i.then_inc(q["out_ps"], 1)

                def body(j, u, has):
                    now, nxt = tile_at(j, u, 0), tile_at(j, u, 1)
                    if has(1):
                        transpose_h(*nxt)
                        similarities(*nxt)
                        experts(*nxt)
                        gate_up(*nxt)
                    if has(0):
                        mlp_out(*now)
                        transpose_w(*now, has(1))
                        experts_out(*now)

                steps(pe, body, NB, 2, 1)


_WEIGHTS = None


def kernel(**inputs):
    import numpy as np
    import concourse.bacc as bacc
    from concourse.bass_utils import run_bass_kernel_spmd

    a = {k.replace("L0_", ""): np.asarray(v) for k, v in inputs.items()}

    def rows(w):
        return np.ascontiguousarray(w.reshape(-1, 128, w.shape[1]).transpose(1, 0, 2))

    def cols(b):
        return np.ascontiguousarray(b.reshape(-1, 128).T)

    n = IMG // P
    patches = a["x"].reshape(B, CH, n, P, n, P).transpose(0, 2, 4, 3, 5, 1).reshape(B, NP_, PD)
    x = np.zeros((NA, C, PD), np.float32)
    for t in range(NA):
        for g in range(G):
            x[t, g * S + 1:(g + 1) * S] = patches[min(G * t, B - G) + g]

    image = np.zeros((G, C), np.float32)
    for g in range(G):
        image[g, g * S:(g + 1) * S] = 1.0
    image_q = image.copy()
    image_q[0, R] = 1.0
    ones = np.ones((1, C), np.float32)
    far, near_k, near_q = -BIG * ones, BIG * image, BIG * image_q
    mask = np.concatenate([
        np.concatenate([ones, image_q]), np.concatenate([ones, image]),
        np.tile(np.concatenate([far, near_k]), (1, HB)), np.tile(np.concatenate([far, near_q]), (1, HB)),
    ], axis=1)
    feeds = {
        "x": x,
        "ident": np.eye(128, dtype=np.float32),
        "nident": -np.eye(C, dtype=np.float32),
        "headmask": np.kron(np.eye(HC, dtype=np.float32), np.ones((DK, 1), np.float32)),
        "mask": mask,
        "ln1_w": cols(a["tok_ln1_w"]), "ln1_b": cols(a["tok_ln1_b"]),
        "lin_w": rows(a["tok_lin_w"]), "lin_b": a["tok_lin_b"][None],
        "ln2_w": a["tok_ln2_w"][None], "ln2_b": a["tok_ln2_b"][None],
        "cls": a["tok_cls_token"][0], "pos": a["tok_pos_embedding"][0],
        "wq": rows(a["attn_Wq"].T), "wk": rows(a["attn_Wk"].T), "wv": rows(a["attn_Wv"].T),
        "wo": rows(a["attn_Wo"].T),
        "bq": cols(a["attn_bq"]), "bk": cols(a["attn_bk"]),
        "bv": a["attn_bv"][None], "bo": a["attn_bo"][None],
        "wg": rows(a["ffn_Wg"]), "wu": rows(a["ffn_Wu"]), "wd": rows(a["ffn_Wd"]),
        "bg": cols(a["ffn_bg"]), "bu": cols(a["ffn_bu"]), "bd": a["ffn_bd"][None],
        "wqf": np.ascontiguousarray(a["ffn_Wq"].reshape(D, 2 * PH, RET).transpose(2, 1, 0)),
        "keys": np.ascontiguousarray(a["ffn_keys"].transpose(3, 2, 0, 1).reshape(RET, 2 * PH, NK)),
        "down": rows(a["ffn_down_embed"].T), "up": rows(a["ffn_up_embed"]),
    }
    feeds = {f"in_{k}": np.ascontiguousarray(v) for k, v in feeds.items()}
    nc = bacc.Bacc("TRN2", target_bir_lowering=False, num_devices=1)
    args = {k[3:]: nc.dram_tensor(k, v.shape, F32, kind="ExternalInput").ap() for k, v in feeds.items()}
    out = nc.dram_tensor("out", (N, D), F32, kind="ExternalOutput").ap()
    h1_dram = nc.dram_tensor("h1_dram", (N, D), F32, kind="Internal").ap()
    vit_tower(nc, args, out, h1_dram)
    r = run_bass_kernel_spmd(nc, [feeds], core_ids=[0])
    return r.results[0]["out"].reshape(B, S, D)
```

```python
from contextlib import ExitStack

import concourse.bass as bass
from concourse import mybir

F32 = mybir.dt.float32
F32R = mybir.dt.float32r
BF16 = mybir.dt.bfloat16
ALU = mybir.AluOpType
ACT = mybir.ActivationFunctionType
AX = mybir.AxisListType.X

B, CH, IMG, P = 64, 3, 96, 16
NP_ = (IMG // P) ** 2
S = NP_ + 1
PD = P * P * CH
D = 256
H, DK = 16, 16
G = 3
R = G * S
C = R + 1
NA = -(-B // G)
KP = PD // 128
KD = D // 128
HC = H // KD
HB = H // 4
N = B * S
NB = -(-N // 128)
F = 1024
KF = F // 128
PH, NK, RET = 4, 64, 64
NE = 1024
XR = NE // NK
T8 = 8
EPS = 1e-5
BIG = 65536.0


def late(t, n):
    return not isinstance(t, int) or t >= n


def steps(engine, body, n, ahead, behind):
    first = -ahead
    lo = 4
    hi = n - ahead
    hi -= (hi - lo) % 2
    for t in range(first, lo):
        body(t // 2, t % 2, lambda k, t=t: 0 <= t + k < n)
    with engine.Fori(lo // 2, hi // 2) as j:
        for u in (0, 1):
            body(j, u, lambda k: True)
    for t in range(hi, n + behind):
        body(t // 2, t % 2, lambda k, t=t: 0 <= t + k < n)


def tile_at(j, u, k):
    q = u + k
    return 2 * j + q, j + q // 2, q % 2


def vit_tower(nc, I, out, h1_dram):
    with ExitStack() as ctx:
        def sb(name, shape, dt=F32):
            return ctx.enter_context(nc.sbuf_tensor(name, shape, dt))

        def sem(name):
            return ctx.enter_context(nc.semaphore(name))

        ident = sb("ident", [128, 128])
        nident = sb("nident", [C, C])
        headmask = sb("headmask", [128, HC])
        lin_w = sb("lin_w", [128, KP, D])
        ln1_w = sb("ln1_w", [128, KP])
        ln1_b = sb("ln1_b", [128, KP])
        ln1_b_rep = sb("ln1_b_rep", [128, KP, C])
        lin_bias = sb("lin_bias", [C, D])
        ln2_w = sb("ln2_w", [C, D])
        pos = sb("pos", [C, D])
        pos_add = sb("pos_add", [C, D])
        wq = sb("wq", [128, KD, D])
        wk = sb("wk", [128, KD, D])
        wv = sb("wv", [128, KD, D])
        wo = sb("wo", [128, KD, D])
        bq = sb("bq", [128, KD])
        bk = sb("bk", [128, KD])
        bv = sb("bv", [C, D])
        bo = sb("bo", [C, D])
        mask_f = sb("mask_f", [4, 2 * C + 2 * HB * C])
        mask_b = sb("mask_b", [4, 2 * C + 2 * HB * C], BF16)
        sum_lhs = sb("sum_lhs", [C + 4, C], BF16)
        eps = sb("eps", [128, 1])
        mhalf = sb("mhalf", [128, 1])
        minus_one = sb("minus_one", [128, 1])
        wg = sb("wg", [128, KD, F])
        wu = sb("wu", [128, KD, F])
        wd = sb("wd", [128, KF, D])
        bg = sb("bg", [128, KF])
        bu = sb("bu", [128, KF])
        bd = sb("bd", [128, D])
        wqf = sb("wqf", [RET, 2 * PH, D])
        keys = sb("keys", [RET, 2 * PH, NK])
        simw = sb("simw", [128, KD, 2 * PH * NK])
        simw_hi = sb("simw_hi", [128, KD, 2 * PH * NK], F32R)
        simw_lo = sb("simw_lo", [128, KD, 2 * PH * NK], F32R)
        down = sb("down", [128, KD, NE])
        up = sb("up", [128, NE // 128, D])
        hx = sb("hx", [128, 2, D])

        w_lin = sem("w_lin")
        w_a = sem("w_a")
        w_sim = sem("w_sim")
        w_b = sem("w_b")
        w_b2 = sem("w_b2")
        const_f = sem("const_f")
        const_c = sem("const_c")
        mask_ready = sem("mask_ready")
        mask_moved = sem("mask_moved")
        rep_ready = sem("rep_ready")
        bias_ready = sem("bias_ready")
        heads_ready = sem("heads_ready")
        fold_ready = sem("fold_ready")
        lin_hi_ready = sem("lin_hi_ready")
        lin_lo_ready = sem("lin_lo_ready")
        simw_hi_ready = sem("simw_hi_ready")
        bias_ps = sem("bias_ps")
        pos_ready = sem("pos_ready")
        pos_zero = sem("pos_zero")
        h1_stored = [sem("h1_stored0"), sem("h1_stored1")]
        h_loaded = [sem("h_loaded0"), sem("h_loaded1")]
        simw_ps = sem("simw_ps")
        simw_ready = sem("simw_ready")

        stf = sb("stf", [128, 2, 6])
        mvf = sb("mvf", [128, 2, 2])
        vef = sb("vef", [128, 1])
        rstdf = sb("rstdf", [128, 2])
        hf = sb("hf", [128, D])
        hfT = sb("hfT", [128, KD, 128])
        hfT_hi = sb("hfT_hi", [128, KD, 128], F32R)
        hfT_lo = sb("hfT_lo", [128, KD, 128], F32R)
        sims = sb("sims", [128, 2, 2, PH, NK])
        gate = sb("gate", [128, 2, KF, 128])
        gate_t = sb("gate_t", [128, 2, KF, 128])
        de_t = sb("de_t", [128, NE // 128, 128])
        top = sb("top", [128, 2, PH, T8])
        grid = sb("grid", [128, PH, T8, T8])
        best = sb("best", [128, PH, T8])
        rel = sb("rel", [128, PH, T8])
        neg_m = sb("neg_m", [128, PH])

        def ps(name, shape):
            return ctx.enter_context(nc.psum_tensor(name, shape, F32))

        ps_x = ps("ps_x", [128, 512])
        ps_yl = ps("ps_yl", [128, 2, 512])
        ps_y = ps_yl[:, 0, :]
        ps_l = ps_yl[:, 1, :]
        ps_o = ps("ps_o", [128, 512])
        ps_s = ps("ps_s", [128, 4, 512])
        ps_m, ps_e, ps_out = ps_x, ps_yl, ps_o
        ps_g = ps_s[:, 0:2, :]
        ps_u = ps_s[:, 2:4, :]

        b_names = ("stf_ready mvf_ready vef_ready rstdf_ready hf_ready hxb_ready hfT_ps hfT_ready hi_ready lo_ready "
                   "sim_ps sims_ready e_ps e_tanh gate_ps up_ps gate_ready gate_t_ready up_ready "
                   "silu_ready top_ready grid_ready best_ready rel_ready negm_ready erel_ready z_ready "
                   "rz_ready pair_ready exp_ready epair_ready picked_ready act_ready hid_ready "
                   "coef_ready half_ready sum_ready coefT_ps wT_ready out_ps res_ready "
                   "const_ready neg_mean_ready shift_ready stored0 stored1").split()
        q = {n: sem("b_" + n) for n in b_names}

        def by_feature(pe, ps, w, ms):
            for m in ms:
                for k in range(KD):
                    i = pe.matmul(ps[:, m // 4, (m % 4) * 128:(m % 4 + 1) * 128],
                                  w[:, k, m * 128:(m + 1) * 128], hfT[:, k, :], start=k == 0, stop=k == KD - 1)
            return i

        def sim_products(pe):
            for k in range(KD):
                pe.matmul(ps_m[:, :], hfT_hi[:, k, :], simw_lo[:, k, :], start=k == 0, stop=False)
                pe.matmul(ps_m[:, :], hfT_hi[:, k, :], simw_hi[:, k, :], start=False, stop=False)
                i = pe.matmul(ps_m[:, :], hfT_lo[:, k, :], simw_hi[:, k, :], start=False, stop=k == KD - 1)
            return i

        def top_keys(dve, t, j, u):
            if isinstance(t, int):
                dve.wait_ge(q["sims_ready"], t + 1)
            for p in range(2):
                for n in range(PH):
                    i = dve.max(top[:, p, n, :], sims[:, u, p, n, :])
            i.then_inc(q["top_ready"], 1)

        def top_pairs(dve, t, j, u):
            dve.wait_ge(q["top_ready"], t + 1)
            dve.tensor_tensor(grid[:, :, :, :],
                              top[:, 0, :, :].unsqueeze(3).to_broadcast([128, PH, T8, T8]),
                              top[:, 1, :, :].unsqueeze(2).to_broadcast([128, PH, T8, T8]),
                              ALU.add).then_inc(q["grid_ready"], 1)

        def best_pairs(dve, t, j, u):
            for n in range(PH):
                i = dve.max(best[:, n, :], grid[:, n, :, :].rearrange("p a b -> p (a b)"))
            i.then_inc(q["best_ready"], 1)

        def relative(dve, t, j, u):
            dve.wait_ge(q["best_ready"], t + 1)
            dve.tensor_scalar(neg_m[:, :], best[:, :, 0], -1.0, None, ALU.mult).then_inc(q["negm_ready"], 1)
            dve.tensor_tensor(rel[:, :, :], best[:, :, :],
                              best[:, :, 0:1].to_broadcast([128, PH, T8]),
                              ALU.subtract).then_inc(q["rel_ready"], 1)

        def expert_tanh(act, t, j, u):
            act.wait_ge(q["e_ps"], t + 1)
            if late(t, 1):
                act.wait_ge(q["silu_ready"], t)
            act.activation(de_t[:, :, :].rearrange("p a b -> p (a b)"),
                           ps_e[:, :, :].rearrange("p a b -> p (a b)"), ACT.Tanh, scale=0.5).then_inc(q["e_tanh"], 1)

        def gates(act, t, j, u):
            act.wait_ge(q["gate_ps"], t + 1)
            for m in range(KF):
                i = act.activation(gate[:, u, m, :], ps_g[:, m // 4, (m % 4) * 128:(m % 4 + 1) * 128],
                                   ACT.Identity, bias=bg[:, m:m + 1])
            i.then_inc(q["gate_ready"], 1)
            act.wait_ge(q["gate_ready"], t + 1)
            act.activation(gate_t[:, u, :, :], gate[:, u, :, :], ACT.Tanh, scale=0.5).then_inc(q["gate_t_ready"], 1)

        with ExitStack() as ca:
            def sa(name, shape, dt=F32):
                return ca.enter_context(nc.sbuf_tensor(name, shape, dt))

            lin_f = sa("lin_f", [128, KP, D])
            lin_hi = sa("lin_hi", [128, KP, D], F32R)
            lin_lo = sa("lin_lo", [128, KP, D], F32R)
            xin = sa("xin", [C, 2, PD])
            xn = sa("xn", [C, 2, PD])
            st1 = sa("st1", [C, 2, 12])
            st2 = sa("st2", [C, 2, 6])
            st3 = sa("st3", [C, 2, 6])
            mv1 = sa("mv1", [C, 2, 2])
            mv2 = sa("mv2", [C, 2, 2])
            mv3 = sa("mv3", [C, 2, 2])
            ve = sa("ve", [C, 3, 1])
            rstd = sa("rstd", [C, 3, 2])
            neg_mean1 = sa("neg_mean1", [C, 1])
            shift1 = sa("shift1", [C, 2])
            xT_hi = sa("xT_hi", [128, KP, C], F32R)
            xT_lo = sa("xT_lo", [128, KP, C], F32R)
            y = sa("y", [C, D])
            yn = sa("yn", [C, D])
            yw = sa("yw", [C, D])
            h = sa("h", [C, 2, D])
            hb = sa("hb", [C, 2, D])
            hn = sa("hn", [C, D])
            hnT = sa("hnT", [128, KD, C])
            qT = sa("qT", [128, KD, C])
            kT = sa("kT", [128, KD, C])
            qTb = sa("qTb", [128, KD, C], BF16)
            kTb = sa("kTb", [128, KD, C], BF16)
            headmask_b = sa("headmask_b", [128, HC, C], BF16)
            q_exp = sa("q_exp", [128, KD, HC, C])
            k_exp = sa("k_exp", [128, KD, HC, C], BF16)
            v_aug = sa("v_aug", [C, 2, H, DK + 1])
            mx = sa("mx", [C, H])
            diag = sa("diag", [C + 4, H, C], BF16)
            pT = sa("pT", [C, H, C])
            rden = sa("rden", [C, H])
            o = sa("o", [C, D])
            oT = sa("oT", [128, KD, C])
            h1 = sa("h1", [C, 2, D])

            x_loaded = [ctx.enter_context(nc.semaphore(f"x_loaded{u}")) for u in (0, 1)]
            st1_ready = sem("st1_ready")
            mv1_ready = sem("mv1_ready")
            st2_ready = sem("st2_ready")
            mv2_ready = sem("mv2_ready")
            st3_ready = sem("st3_ready")
            mv3_ready = sem("mv3_ready")
            ve_ready = [ctx.enter_context(nc.semaphore(f"ve_ready{k}")) for k in range(3)]
            rstd1_ready = sem("rstd1_ready")
            rstd2_ready = sem("rstd2_ready")
            rstd3_ready = sem("rstd3_ready")
            neg_mean1_ready = sem("neg_mean1_ready")
            shift1_ready = sem("shift1_ready")
            xn_ready = sem("xn_ready")
            xT_ps = sem("xT_ps")
            xT_hi_ready = sem("xT_hi_ready")
            xT_ready = sem("xT_ready")
            lin_ps = sem("lin_ps")
            y_ready = sem("y_ready")
            yn_ready = sem("yn_ready")
            yw_ready = sem("yw_ready")
            h_ready = sem("h_ready")
            hb_ready = sem("hb_ready")
            hn_ready = sem("hn_ready")
            hnT_ps = sem("hnT_ps")
            hnT_ready = sem("hnT_ready")
            k_ps = sem("k_ps")
            q_ps = sem("q_ps")
            kb_ready = sem("kb_ready")
            v_ps = sem("v_ps")
            qk_ready = sem("qk_ready")
            qb_ready = sem("qb_ready")
            kexp_ready = sem("kexp_ready")
            qexp_ready = sem("qexp_ready")
            v_ready = sem("v_ready")
            s_ps = sem("s_ps")
            max_ready = sem("max_ready")
            diag_ready = sem("diag_ready")
            st_ps = sem("st_ps")
            p_ready = sem("p_ready")
            pv_ps = sem("pv_ps")
            rden_ready = sem("rden_ready")
            o_ready = sem("o_ready")
            oT_ps = sem("oT_ps")
            oT_ready = sem("oT_ready")
            wo_ps = sem("wo_ps")
            h1_ready = sem("h1_ready")

            block = ca.enter_context(nc.Block())

            loads_lin = [
                (ident[:, :], I["ident"]), (ln1_w[:, :], I["ln1_w"]), (ln1_b[:, :], I["ln1_b"]),
            ]
            loads_a = [(lin_bias[:, :], I["lin_b"].to_broadcast([C, D])), (headmask[:, :], I["headmask"])]
            loads_a2 = [
                (wv[:, :, :], I["wv"]), (wk[:, :, :], I["wk"]), (wq[:, :, :], I["wq"]), (mask_f[:, :], I["mask"]),
                (bk[:, :], I["bk"]), (bq[:, :], I["bq"]), (bv[:, :], I["bv"].to_broadcast([C, D])),
                (nident[:, :], I["nident"]), (bo[:, :], I["bo"].to_broadcast([C, D])), (wo[:, :, :], I["wo"]),
            ]
            loads_rows = []
            for g in range(G):
                loads_rows += [
                    (ln2_w[g * S + 1:(g + 1) * S, :], I["ln2_w"].to_broadcast([NP_, D])),
                    (pos_add[g * S + 1:(g + 1) * S, :], I["ln2_b"].to_broadcast([NP_, D])),
                    (pos_add[g * S:g * S + 1, :], I["cls"]),
                    (pos[g * S:(g + 1) * S, :], I["pos"]),
                ]
            loads_b = [
                (down[:, :, :], I["down"]),
                (wg[:, :, :], I["wg"]), (wu[:, :, :], I["wu"]), (bg[:, :], I["bg"]), (bu[:, :], I["bu"]),
                (wd[:, :, :], I["wd"]), (up[:, :, :], I["up"]), (bd[:, :], I["bd"].to_broadcast([128, D])),
            ]
            n_loads_lin = 16 * (len(loads_lin) + 1)
            n_loads_a = 16 * (len(loads_a) + len(loads_a2))
            n_loads_rows = 16 * len(loads_rows)

            @block.sync
            def _(sp):
                def load_x(t, j, u):
                    if late(t, 2):
                        sp.wait_ge(xn_ready, t - 1)
                    sp.dma_start(xin[:, u, :], I["x"][t, :, :]).then_inc(x_loaded[u], 16)

                def store(t, j, u):
                    sp.wait_ge(h1_ready, t + 1)
                    if isinstance(t, int) and t == NA - 1:
                        new = B - (NA - 1) * G
                        sp.dma_start(h1_dram[(B - new) * S:B * S, :],
                                     h1[R - new * S:R, u, :]).then_inc(h1_stored[u], 16)
                    else:
                        sp.dma_start(h1_dram[bass.ds(t * R, R), :], h1[0:R, u, :]).then_inc(h1_stored[u], 16)

                def body(j, u, has):
                    if has(4) and late(tile_at(j, u, 4)[0], 4):
                        load_x(*tile_at(j, u, 4))
                    if has(-1):
                        store(*tile_at(j, u, -1))
                    if has(1) and not has(2):
                        for v in (0, 1):
                            sp.wait_ge(h1_stored[v], 16 * (2 - v))
                        for v in (0, 1):
                            sp.dma_start(hx[:, v, :], h1_dram[v * 128:(v + 1) * 128, :]).then_inc(h_loaded[v], 16)

                load_x(0, 0, 0)
                sp.dma_start(lin_w[:, :, :], I["lin_w"]).then_inc(w_lin, 16)
                load_x(1, 0, 1)
                for dst, src in ((wqf[:, :, :], I["wqf"]), (keys[:, :, :], I["keys"])):
                    sp.dma_start(dst, src).then_inc(w_sim, 16)
                for dst, src in loads_a2:
                    sp.dma_start(dst, src).then_inc(w_a, 16)
                sp.wait_ge(pos_zero, 3)
                for dst, src in loads_rows:
                    sp.dma_start(dst, src).then_inc(w_b, 16)
                load_x(2, 1, 0)
                load_x(3, 1, 1)
                sp.wait_ge(mask_ready, 1)
                for r in range(H // HB):
                    sp.dma_start(diag[C:C + 4, r * HB:(r + 1) * HB, :],
                                 mask_b[:, 2 * C + HB * C:2 * C + 2 * HB * C]
                                 .rearrange("p (a b) -> p a b", a=HB)).then_inc(mask_moved, 16)
                sp.wait_ge(const_c, 1)
                sp.dma_start(sum_lhs[C:C + 4, :], mask_b[:, C:2 * C]).then_inc(mask_moved, 16)
                for dst, src in loads_b:
                    sp.dma_start(dst, src).then_inc(w_b2, 16)
                steps(sp, body, NA, 4, 1)
                sp.wait_ge(w_b2, 16 * len(loads_b))
                for u in (0, 1):
                    sp.wait_ge(h1_stored[u], 16 * ((NA + 1 - u) // 2))

            @block.gpsimd
            def _(pool):
                pool.memset(ln2_w[:, :], 0.0).then_inc(pos_zero, 1)
                pool.memset(pos_add[:, :], 0.0).then_inc(pos_zero, 1)
                pool.memset(pos[:, :], 0.0).then_inc(pos_zero, 1)
                pool.memset(sum_lhs[:, :], 1.0).then_inc(const_c, 1)
                pool.memset(eps[:, :], EPS).then_inc(const_f, 1)
                pool.memset(mhalf[:, :], -0.5).then_inc(const_f, 1)
                pool.memset(minus_one[:, :], -1.0).then_inc(const_f, 1)
                pool.wait_ge(const_f, 3)

                def make_rstd(k, t, var, dst):
                    pool.tensor_tensor(ve[:, k, :], var, eps[0:C, :], ALU.add).then_inc(ve_ready[k], 1)
                    pool.wait_ge(ve_ready[k], t + 1)
                    return pool.tensor_tensor(dst, ve[:, k, :], mhalf[0:C, :], ALU.pow)

                def body(j, u, has):
                    if has(1):
                        t, _, u1 = tile_at(j, u, 1)
                        pool.wait_ge(mv2_ready, t + 1)
                        make_rstd(1, t, mv2[:, u1, 1:2], rstd[:, 1, u1:u1 + 1]).then_inc(rstd2_ready, 1)
                    if has(0):
                        t = tile_at(j, u, 0)[0]
                        for half in (0, 1):
                            heads = slice(half * H // 2, (half + 1) * H // 2)
                            pool.wait_ge(max_ready, 4 * t + 2 * half + 2)
                            pool.tensor_tensor(diag[0:C, heads, :],
                                               nident[:, :].unsqueeze(1).to_broadcast([C, H // 2, C]),
                                               mx[:, heads].unsqueeze(2).to_broadcast([C, H // 2, C]),
                                               ALU.mult).then_inc(diag_ready, 1)
                    if has(1):
                        t, _, u1 = tile_at(j, u, 1)
                        pool.wait_ge(mv3_ready, t + 1)
                        make_rstd(2, t, mv3[:, u1, 1:2], rstd[:, 2, u1:u1 + 1]).then_inc(rstd3_ready, 1)
                    if has(1):
                        t, _, u1 = tile_at(j, u, 1)
                        if not late(t, 1):
                            pool.wait_ge(w_a, n_loads_a)
                        pool.wait_ge(h_ready, t + 1)
                        if late(t, 2):
                            pool.wait_ge(h1_ready, t - 1)
                        pool.tensor_tensor(hb[:, u1, :], h[:, u1, :], bo[:, :], ALU.add).then_inc(hb_ready, 1)
                    if has(3):
                        t, _, u3 = tile_at(j, u, 3)
                        pool.wait_ge(mv1_ready, t + 1)
                        if late(t, 1):
                            pool.wait_ge(shift1_ready, t)
                        pool.tensor_tensor(neg_mean1[:, :], mv1[:, u3, 0:1], minus_one[0:C, :],
                                           ALU.mult).then_inc(neg_mean1_ready, 1)
                        make_rstd(0, t, mv1[:, u3, 1:2], rstd[:, 0, u3:u3 + 1]).then_inc(rstd1_ready, 1)
                        pool.wait_ge(neg_mean1_ready, t + 1)
                        pool.wait_ge(rstd1_ready, t + 1)
                        if late(t, 2):
                            pool.wait_ge(xn_ready, t - 1)
                        pool.tensor_tensor(shift1[:, u3:u3 + 1], neg_mean1[:, :], rstd[:, 0, u3:u3 + 1],
                                           ALU.mult).then_inc(shift1_ready, 1)

                steps(pool, body, NA, 3, 1)
                for t in (0, 1):
                    pool.wait_ge(q["mvf_ready"], t + 1)
                    pool.tensor_tensor(vef[:, :], mvf[:, t, 1:2], eps[:, :], ALU.add).then_inc(q["vef_ready"], 1)
                    pool.wait_ge(q["vef_ready"], t + 1)
                    pool.tensor_tensor(rstdf[:, t:t + 1], vef[:, :], mhalf[:, :],
                                       ALU.pow).then_inc(q["rstdf_ready"], 1)

            @block.vector
            def _(dve):
                dve.memset(v_aug[:, :, :, :], 1.0).then_inc(heads_ready, 1)

                def fold_gain():
                    dve.wait_ge(w_lin, n_loads_lin)
                    dve.tensor_tensor(lin_f[:, :, :], lin_w[:, :, :],
                                      ln1_w[:, :].unsqueeze(2).to_broadcast([128, KP, D]),
                                      ALU.mult).then_inc(fold_ready, 1)
                    dve.wait_ge(lin_hi_ready, 1)
                    dve.tensor_tensor(lin_lo[:, :, :], lin_f[:, :, :], lin_hi[:, :, :],
                                      ALU.subtract).then_inc(lin_lo_ready, 1)

                def bf16_masks():
                    dve.wait_ge(w_a, n_loads_a)
                    dve.tensor_copy(mask_b[:, :], mask_f[:, :]).then_inc(mask_ready, 1)

                def fold_bias():
                    bf16_masks()
                    dve.wait_ge(bias_ps, 1)
                    dve.tensor_tensor(lin_bias[:, :], ps_o[0:C, 0:D], lin_bias[:, :], ALU.add).then_inc(bias_ready, 1)
                    dve.wait_ge(bias_ready, 1)

                def positions():
                    dve.wait_ge(w_b, n_loads_rows)
                    dve.tensor_tensor(pos_add[:, :], pos_add[:, :], pos[:, :], ALU.add).then_inc(pos_ready, 1)
                    dve.wait_ge(pos_ready, 1)

                def head_masks():
                    dve.wait_ge(w_a, n_loads_a)
                    dve.tensor_copy(headmask_b[:, :, :],
                                    headmask[:, :].unsqueeze(2).to_broadcast([128, HC, C])).then_inc(heads_ready, 1)
                    dve.wait_ge(heads_ready, 2)

                def aggregate(ready, mv, st, done, t, u):
                    if isinstance(t, int):
                        dve.wait_ge(ready, t + 1)
                    dve.bn_aggr(mv[:, u, :], st[:, u, :]).then_inc(done, 1)

                def normaliser(t, j, u):
                    if not isinstance(t, int):
                        dve.wait_ge(st2_ready, t + 3)
                    dve.wait_ge(pv_ps, t + 1)
                    pv = ps_o[0:C, 0:H * (DK + 1)].rearrange("p (h d) -> p h d", h=H)
                    dve.reciprocal(rden[:, :], pv[:, :, DK]).then_inc(rden_ready, 1)

                def normalise(t, j, u):
                    dve.wait_ge(rden_ready, t + 1)
                    pv = ps_o[0:C, 0:H * (DK + 1)].rearrange("p (h d) -> p h d", h=H)
                    dve.tensor_tensor(o[:, :].rearrange("p (h d) -> p h d", h=H), pv[:, :, 0:DK],
                                      rden[:, :].unsqueeze(2).to_broadcast([C, H, DK]),
                                      ALU.mult).then_inc(o_ready, 1)

                def row_max(t, j, u):
                    for b in range(4):
                        dve.wait_ge(s_ps, 4 * t + b + 1)
                        dve.tensor_reduce(mx[:, b * HB:(b + 1) * HB],
                                          ps_s[0:C, b, 0:HB * C].rearrange("p (h k) -> p h k", h=HB),
                                          AX, ALU.max).then_inc(max_ready, 1)

                def residual(t, j, u):
                    dve.wait_ge(wo_ps, t + 1)
                    dve.wait_ge(hb_ready, t + 1)
                    if late(t, 2):
                        dve.wait_ge(h1_stored[u], 16 * j)
                    dve.tensor_tensor(h1[:, u, :], ps_o[0:C, 0:D], hb[:, u, :], ALU.add).then_inc(h1_ready, 1)

                def stats1(t, j, u):
                    dve.wait_ge(x_loaded[u], 16 * (j + 1))
                    dve.bn_stats(st1[:, u, 0:6], xin[:, u, 0:PD // 2])
                    dve.bn_stats(st1[:, u, 6:12], xin[:, u, PD // 2:PD]).then_inc(st1_ready, 1)

                def norm1_first():
                    dve.wait_ge(rstd1_ready, 1)
                    dve.tensor_scalar(xn[:, 0, :], xin[:, 0, :], mv1[:, 0, 0:1], rstd[:, 0, 0:1],
                                      ALU.subtract, ALU.mult).then_inc(xn_ready, 1)
                    fold_gain()

                def embed(t, j, u):
                    if not late(t, 1):
                        fold_bias()
                    dve.wait_ge(lin_ps, t + 1)
                    dve.tensor_tensor(y[:, :], ps_l[0:C, 0:D], lin_bias[:, :], ALU.add).then_inc(y_ready, 1)
                    dve.wait_ge(y_ready, t + 1)
                    dve.bn_stats(st2[:, u, :], y[:, :]).then_inc(st2_ready, 1)

                def split_xT(t, j, u, part):
                    ks, ps = ((slice(0, 4), ps_x), (slice(4, KP), ps_y))[part]
                    n = ks.stop - ks.start
                    dve.wait_ge(xT_hi_ready, t + 1)
                    if late(t, 1):
                        dve.wait_ge(lin_ps, t)
                    if part == 1 and not isinstance(t, int):
                        dve.wait_ge(st3_ready, t)
                    dve.tensor_tensor(xT_lo[:, ks, :], ps[:, 0:n * C].rearrange("p (k c) -> p k c", k=n),
                                      xT_hi[:, ks, :], ALU.subtract).then_inc(xT_ready, 1)

                def layer_norm2(t, j, u):
                    dve.wait_ge(rstd2_ready, t + 1)
                    dve.tensor_scalar(yn[:, :], y[:, :], mv2[:, u, 0:1], rstd[:, 1, u:u + 1],
                                      ALU.subtract, ALU.mult).then_inc(yn_ready, 1)

                def weigh(t, j, u):
                    if not late(t, 1):
                        positions()
                    dve.wait_ge(yn_ready, t + 1)
                    dve.tensor_tensor(yw[:, :], yn[:, :], ln2_w[:, :], ALU.mult).then_inc(yw_ready, 1)

                def tokens(t, j, u):
                    dve.wait_ge(yw_ready, t + 1)
                    dve.tensor_tensor(h[:, u, :], yw[:, :], pos_add[:, :], ALU.add).then_inc(h_ready, 1)
                    dve.wait_ge(h_ready, t + 1)
                    dve.bn_stats(st3[:, u, :], h[:, u, :]).then_inc(st3_ready, 1)

                def norm3(t, j, u):
                    dve.wait_ge(rstd3_ready, t + 1)
                    dve.tensor_scalar(hn[:, :], h[:, u, :], mv3[:, u, 0:1], rstd[:, 2, u:u + 1],
                                      ALU.subtract, ALU.mult).then_inc(hn_ready, 1)

                def copy_hnT(t, j, u):
                    dve.wait_ge(hnT_ps, t + 1)
                    dve.tensor_copy(hnT[:, :, :],
                                    ps_y[:, 0:KD * C].rearrange("p (k c) -> p k c", k=KD)).then_inc(hnT_ready, 1)

                def values(t, j, u):
                    if not late(t, 1):
                        head_masks()
                    dve.wait_ge(v_ps, t + 1)
                    if not isinstance(t, int):
                        dve.wait_ge(st1_ready, t + 3)
                    dve.tensor_tensor(v_aug[:, u, :, 0:DK],
                                      ps_o[0:C, 0:D].rearrange("p (h d) -> p h d", h=H),
                                      bv[:, :].rearrange("p (h d) -> p h d", h=H), ALU.add).then_inc(v_ready, 1)

                def expand_k(t, j, u):
                    dve.wait_ge(kb_ready, t + 1)
                    for c in range(KD):
                        i = dve.tensor_tensor(k_exp[:, c, :, :], kTb[:, c, :].unsqueeze(1).to_broadcast([128, HC, C]),
                                              headmask_b[:, :, :], ALU.mult)
                    i.then_inc(kexp_ready, 1)

                def expand_q(t, j, u):
                    dve.wait_ge(qk_ready, t + 1)
                    for c in range(KD):
                        i = dve.tensor_tensor(q_exp[:, c, :, :], qT[:, c, :].unsqueeze(1).to_broadcast([128, HC, C]),
                                              headmask[:, :].unsqueeze(2).to_broadcast([128, HC, C]), ALU.mult)
                    i.then_inc(qexp_ready, 1)

                def best_of_phase_b():
                    top_keys(dve, 0, 0, 0)
                    top_pairs(dve, 0, 0, 0)
                    dve.wait_ge(q["grid_ready"], 1)
                    best_pairs(dve, 0, 0, 0)
                    relative(dve, 0, 0, 0)

                def first_of_phase_b():
                    dve.wait_ge(h_loaded[0], 16)
                    dve.bn_stats(stf[:, 0, :], hx[:, 0, :]).then_inc(q["stf_ready"], 1)
                    dve.wait_ge(q["stf_ready"], 1)
                    dve.bn_aggr(mvf[:, 0, :], stf[:, 0, :]).then_inc(q["mvf_ready"], 1)
                    dve.wait_ge(q["rstdf_ready"], 1)
                    dve.tensor_scalar(hf[:, :], hx[:, 0, :], mvf[:, 0, 0:1], rstdf[:, 0:1],
                                      ALU.subtract, ALU.mult).then_inc(q["hf_ready"], 1)
                    dve.wait_ge(simw_hi_ready, 1)
                    dve.tensor_tensor(simw_lo[:, :, :], simw[:, :, :], simw_hi[:, :, :],
                                      ALU.subtract).then_inc(simw_ready, 1)
                    dve.wait_ge(q["hi_ready"], 1)
                    dve.wait_ge(q["hfT_ready"], 1)
                    dve.tensor_tensor(hfT_lo[:, :, :], hfT[:, :, :], hfT_hi[:, :, :],
                                      ALU.subtract).then_inc(q["lo_ready"], 1)
                    dve.wait_ge(h_loaded[1], 16)
                    dve.bn_stats(stf[:, 1, :], hx[:, 1, :]).then_inc(q["stf_ready"], 1)
                    dve.wait_ge(q["stf_ready"], 2)
                    dve.bn_aggr(mvf[:, 1, :], stf[:, 1, :]).then_inc(q["mvf_ready"], 1)
                    dve.wait_ge(q["rstdf_ready"], 2)
                    dve.wait_ge(q["hfT_ps"], 1)
                    dve.tensor_scalar(hf[:, :], hx[:, 1, :], mvf[:, 1, 0:1], rstdf[:, 1:2],
                                      ALU.subtract, ALU.mult).then_inc(q["hf_ready"], 1)

                def body(j, u, has):
                    t1, u1 = tile_at(j, u, 1)[::2]
                    t3, u3 = tile_at(j, u, 3)[::2]
                    if has(1):
                        embed(*tile_at(j, u, 1))
                    if has(-1):
                        normaliser(*tile_at(j, u, -1))
                    if has(1):
                        aggregate(st2_ready, mv2, st2, mv2_ready, t1, u1)
                    if has(-1):
                        normalise(*tile_at(j, u, -1))
                    if has(-1) and not has(0):
                        best_of_phase_b()
                    if has(0):
                        row_max(*tile_at(j, u, 0))
                    if has(1):
                        layer_norm2(*tile_at(j, u, 1))
                    if has(2):
                        split_xT(*tile_at(j, u, 2), 0)
                    if has(1):
                        weigh(*tile_at(j, u, 1))
                        tokens(*tile_at(j, u, 1))
                    if has(2):
                        split_xT(*tile_at(j, u, 2), 1)
                    if has(1):
                        aggregate(st3_ready, mv3, st3, mv3_ready, t1, u1)
                    if has(-1):
                        residual(*tile_at(j, u, -1))
                    if has(0) and not has(1):
                        first_of_phase_b()
                    if has(1):
                        norm3(*tile_at(j, u, 1))
                        copy_hnT(*tile_at(j, u, 1))
                    if has(3):
                        stats1(*tile_at(j, u, 3))
                    if has(1):
                        values(*tile_at(j, u, 1))
                    if has(3):
                        aggregate(st1_ready, mv1, st1, mv1_ready, t3, u3)
                    if has(1):
                        expand_k(*tile_at(j, u, 1))
                    if has(3) and not late(t3, 1):
                        norm1_first()
                    if has(1):
                        expand_q(*tile_at(j, u, 1))

                steps(dve, body, NA, 3, 1)

            @block.scalar
            def _(act):
                def copy_xT(t, j, u):
                    act.wait_ge(xT_ps, t + 1)
                    if late(t, 1):
                        act.wait_ge(lin_ps, t)
                    act.activation(xT_hi[:, 0:4, :], ps_x[:, 0:4 * C].rearrange("p (k c) -> p k c", k=4), ACT.Copy)
                    act.activation(xT_hi[:, 4:KP, :], ps_y[:, 0:2 * C].rearrange("p (k c) -> p k c", k=2),
                                   ACT.Copy).then_inc(xT_hi_ready, 1)
                    if late(t, 1) and not late(t, 2):
                        act.wait_ge(simw_ps, 1)
                        act.activation(simw[:, :, :], ps_s[:, 0:KD, :], ACT.Copy)
                        act.activation(simw_hi[:, :, :], ps_s[:, 0:KD, :], ACT.Copy).then_inc(simw_hi_ready, 1)

                def norm1(t, j, u):
                    act.wait_ge(shift1_ready, t + 1)
                    if late(t, 2):
                        act.wait_ge(xT_ps, t - 1)
                    act.activation(xn[:, u, :], xin[:, u, :], ACT.Identity, bias=shift1[:, u:u + 1],
                                   scale=rstd[:, 0, u:u + 1]).then_inc(xn_ready, 1)

                def copy_oT(t, j, u):
                    act.wait_ge(oT_ps, t + 1)
                    act.activation(oT[:, :, :], ps_o[:, 0:KD * C].rearrange("p (k c) -> p k c", k=KD),
                                   ACT.Copy).then_inc(oT_ready, 1)

                def exp_scores(t, j, u):
                    for b in range(4):
                        act.wait_ge(st_ps, 4 * t + b + 1)
                        i = act.activation(pT[:, b * HB:(b + 1) * HB, :],
                                           ps_s[0:C, b, 0:HB * C].rearrange("p (h q) -> p h q", h=HB),
                                           ACT.Exp, scale=float(DK) ** -0.5)
                    i.then_inc(p_ready, 1)

                def copy_qk(t, j, u):
                    if not late(t, 1):
                        act.wait_ge(w_a, n_loads_a)
                    act.wait_ge(k_ps, t + 1)
                    if late(t, 1):
                        act.wait_ge(qexp_ready, t)
                    for c in range(KD):
                        i = act.activation(kTb[:, c, :], ps_x[:, c * C:(c + 1) * C], ACT.Identity,
                                           bias=bk[:, c:c + 1])
                    i.then_inc(kb_ready, 1)
                    for c in range(KD):
                        act.activation(kT[:, c, :], ps_x[:, c * C:(c + 1) * C], ACT.Identity,
                                       bias=bk[:, c:c + 1])
                    act.wait_ge(q_ps, t + 1)
                    for c in range(KD):
                        i = act.activation(qT[:, c, :], ps_y[:, c * C:(c + 1) * C], ACT.Identity,
                                           bias=bq[:, c:c + 1])
                    i.then_inc(qk_ready, 1)
                    act.wait_ge(qk_ready, t + 1)
                    act.activation(qTb[:, :, :], qT[:, :, :], ACT.Copy).then_inc(qb_ready, 1)

                def body(j, u, has):
                    if has(-1):
                        copy_oT(*tile_at(j, u, -1))
                    if has(2):
                        copy_xT(*tile_at(j, u, 2))
                    if has(0):
                        exp_scores(*tile_at(j, u, 0))
                    if has(0) and not has(1):
                        act.wait_ge(q["hfT_ps"], 1)
                        act.activation(hfT[:, :, :], ps_m[:, 0:D].rearrange("p (k c) -> p k c", k=KD),
                                       ACT.Copy).then_inc(q["hfT_ready"], 1)
                        act.activation(hfT_hi[:, :, :], ps_m[:, 0:D].rearrange("p (k c) -> p k c", k=KD),
                                       ACT.Copy).then_inc(q["hi_ready"], 1)
                    if has(1):
                        copy_qk(*tile_at(j, u, 1))
                    if has(3) and late(tile_at(j, u, 3)[0], 1):
                        norm1(*tile_at(j, u, 3))

                for dst, src in loads_lin:
                    act.dma_start(dst, src).then_inc(w_lin, 16)
                for dst, src in loads_a:
                    act.dma_start(dst, src).then_inc(w_a, 16)
                act.wait_ge(w_lin, n_loads_lin)
                act.activation(ln1_b_rep[:, :, :], ln1_b[:, :].unsqueeze(2).to_broadcast([128, KP, C]),
                               ACT.Copy).then_inc(rep_ready, 1)
                act.wait_ge(fold_ready, 1)
                act.activation(lin_hi[:, :, :], lin_f[:, :, :], ACT.Copy).then_inc(lin_hi_ready, 1)
                steps(act, body, NA, 3, 1)
                act.wait_ge(q["sim_ps"], 1)
                act.activation(sims[:, 0, :, :, :].rearrange("p a b c -> p (a b c)"), ps_m[:, :],
                               ACT.Copy).then_inc(q["sims_ready"], 1)
                expert_tanh(act, 0, 0, 0)
                gates(act, 0, 0, 0)

            @block.tensor
            def _(pe):
                def bias_product():
                    pe.wait_ge(rep_ready, 1)
                    for k in range(KP):
                        i = pe.matmul(ps_o[0:C, 0:D], ln1_b_rep[:, k, :], lin_w[:, k, :],
                                      start=k == 0, stop=k == KP - 1)
                    i.then_inc(bias_ps, 1)

                def transpose_x(t, j, u):
                    if not late(t, 1):
                        pe.wait_ge(w_lin, n_loads_lin)
                    pe.wait_ge(xn_ready, t + 1)
                    if late(t, 2):
                        pe.wait_ge(qk_ready, t - 1)
                    for k in range(KP):
                        dst = ps_x[:, k * C:(k + 1) * C] if k < 4 else ps_y[:, (k - 4) * C:(k - 3) * C]
                        i = pe.transpose(dst, xn[:, u, k * 128:(k + 1) * 128], ident[0:C, 0:C])
                    i.then_inc(xT_ps, 1)
                    if not late(t, 1):
                        bias_product()
                    elif not late(t, 2):
                        fold_similarities()

                def transpose_o(t, j, u):
                    pe.wait_ge(o_ready, t + 1)
                    for k in range(KD):
                        i = pe.transpose(ps_o[:, k * C:(k + 1) * C], o[:, k * 128:(k + 1) * 128], ident[0:C, 0:C])
                    i.then_inc(oT_ps, 1)

                def scores_for_max(t, j, u):
                    if not late(t, 1):
                        pe.wait_ge(mask_moved, 16 * (H // HB + 1))
                        pe.wait_ge(simw_hi_ready, 1)
                    pe.wait_ge(kexp_ready, t + 1)
                    pe.wait_ge(qb_ready, t + 1)
                    if late(t, 1):
                        pe.wait_ge(p_ready, t)
                    for b in range(4):
                        c, s0 = b // 2, (b % 2) * HB
                        pe.matmul(ps_s[0:C, b, 0:HB * C], qTb[:, c, :], k_exp[:, c, s0:s0 + HB, :],
                                  start=True, stop=False)
                        pe.matmul(ps_s[0:C, b, 0:HB * C], mask_b[:, 0:C], mask_b[:, 2 * C:2 * C + HB * C],
                                  start=False, stop=True).then_inc(s_ps, 1)

                def project_o(t, j, u):
                    pe.wait_ge(oT_ready, t + 1)
                    for k in range(KD):
                        i = pe.matmul(ps_o[0:C, 0:D], oT[:, k, :], wo[:, k, :], start=k == 0, stop=k == KD - 1)
                    i.then_inc(wo_ps, 1)

                def scores(t, j, u):
                    pe.wait_ge(qexp_ready, t + 1)
                    for b in range(4):
                        c, s0 = b // 2, (b % 2) * HB
                        pe.wait_ge(max_ready, 4 * t + b + 1)
                        pe.matmul(ps_s[0:C, b, 0:HB * C], kT[:, c, :], q_exp[:, c, s0:s0 + HB, :],
                                  start=True, stop=False)

                def transpose_hn(t, j, u, has_next):
                    if has_next:
                        pe.wait_ge(xT_ready, 2 * t + 4)
                    pe.wait_ge(hn_ready, t + 1)
                    for k in range(KD):
                        i = pe.transpose(ps_y[:, k * C:(k + 1) * C], hn[:, k * 128:(k + 1) * 128], ident[0:C, 0:C])
                    i.then_inc(hnT_ps, 1)

                def shift(t, j, u):
                    for b in range(4):
                        if b % 2 == 0:
                            pe.wait_ge(diag_ready, 2 * t + b // 2 + 1)
                        pe.matmul(ps_s[0:C, b, 0:HB * C], sum_lhs[:, :], diag[:, b * HB:(b + 1) * HB, :],
                                  start=False, stop=True).then_inc(st_ps, 1)

                def project_v(t, j, u):
                    pe.wait_ge(hnT_ready, t + 1)
                    if not late(t, 1):
                        pe.wait_ge(w_a, n_loads_a)
                        pe.wait_ge(bias_ready, 1)
                    if late(t, 2):
                        pe.wait_ge(h1_ready, t - 1)
                    for k in range(KD):
                        i = pe.matmul(ps_o[0:C, 0:D], hnT[:, k, :], wv[:, k, :], start=k == 0, stop=k == KD - 1)
                    i.then_inc(v_ps, 1)

                def project(w, ps, m, done):
                    for k in range(KD):
                        i = pe.matmul(ps[:, m * C:(m + 1) * C], w[:, k, m * 128:(m + 1) * 128], hnT[:, k, :],
                                      start=k == 0, stop=k == KD - 1)
                    if m == KD - 1:
                        i.then_inc(done, 1)

                def fold_similarities():
                    pe.wait_ge(w_sim, 32)
                    for k in range(KD):
                        for n in range(2 * PH):
                            i = pe.matmul(ps_s[:, k, n * NK:(n + 1) * NK], wqf[:, n, k * 128:(k + 1) * 128],
                                          keys[:, n, :], start=True, stop=True)
                    i.then_inc(simw_ps, 1)

                def transpose_first():
                    pe.wait_ge(q["hf_ready"], 1)
                    for k in range(KD):
                        i = pe.transpose(ps_m[:, k * 128:(k + 1) * 128], hf[:, k * 128:(k + 1) * 128], ident[:, :])
                    i.then_inc(q["hfT_ps"], 1)

                def linear(t, k):
                    if k == 0:
                        pe.wait_ge(xT_ready, 2 * t + 2)
                        if late(t, 1):
                            pe.wait_ge(y_ready, t)
                        else:
                            pe.wait_ge(lin_lo_ready, 1)
                    pe.matmul(ps_l[0:C, 0:D], xT_hi[:, k, :], lin_lo[:, k, :], start=k == 0, stop=False)
                    pe.matmul(ps_l[0:C, 0:D], xT_hi[:, k, :], lin_hi[:, k, :], start=False, stop=False)
                    i = pe.matmul(ps_l[0:C, 0:D], xT_lo[:, k, :], lin_hi[:, k, :], start=False, stop=k == KP - 1)
                    if k == KP - 1:
                        i.then_inc(lin_ps, 1)

                def weighted_values(t, u, n, has_next):
                    if n == 0:
                        pe.wait_ge(p_ready, t + 1)
                        if has_next:
                            pe.wait_ge(v_ready, t + 2)
                        else:
                            pe.wait_ge(v_ready, t + 1)
                            pe.wait_ge(h1_ready, t)
                    i = pe.matmul(ps_o[0:C, n * (DK + 1):(n + 1) * (DK + 1)], pT[:, n, :],
                                  v_aug[:, u, n, :], start=True, stop=True)
                    if n == H - 1:
                        i.then_inc(pv_ps, 1)

                def body(j, u, has):
                    if has(0):
                        scores_for_max(*tile_at(j, u, 0))
                    if has(-1):
                        transpose_o(*tile_at(j, u, -1))
                    if has(2):
                        transpose_x(*tile_at(j, u, 2))
                    if has(-1):
                        project_o(*tile_at(j, u, -1))
                    if has(0):
                        scores(*tile_at(j, u, 0))
                        shift(*tile_at(j, u, 0))
                    t0, t2 = tile_at(j, u, 0)[0], tile_at(j, u, 2)[0]
                    last = has(0) and not has(1)
                    if last:
                        transpose_first()
                        pe.wait_ge(w_b2, 16 * len(loads_b))
                        pe.wait_ge(q["hfT_ready"], 1)
                        by_feature(pe, ps_e, down, range(4))
                    if has(2):
                        linear(t2, 0)
                    if has(1):
                        transpose_hn(*tile_at(j, u, 1), has(2))
                    if has(2):
                        linear(t2, 1)
                        linear(t2, 2)
                    if has(1):
                        project_v(*tile_at(j, u, 1))
                        for m in range(KD):
                            project(wk, ps_x, m, k_ps)
                        for m in range(KD):
                            project(wq, ps_y, m, q_ps)
                    for k in range(2, KP):
                        if has(2) and k > 2:
                            linear(t2, k)
                        if has(0):
                            for n in range((k - 2) * H // (KP - 2), (k - 1) * H // (KP - 2)):
                                weighted_values(t0, u, n, has(1))
                                if last and n % 4 == 1:
                                    i = by_feature(pe, ps_e, down, (4 + n // 4,))
                    if last:
                        i.then_inc(q["e_ps"], 1)

                def body_after(j, u, has):
                    last = tile_at(j, u, -1)
                    pe.wait_ge(q["hi_ready"], 1)
                    pe.wait_ge(q["lo_ready"], 1)
                    pe.wait_ge(simw_ready, 1)
                    sim_products(pe).then_inc(q["sim_ps"], 1)
                    transpose_o(*last)
                    by_feature(pe, ps_g, wg, range(KF)).then_inc(q["gate_ps"], 1)
                    project_o(*last)
                    by_feature(pe, ps_u, wu, range(KF)).then_inc(q["up_ps"], 1)

                steps(pe, body, NA, 3, 0)
                body_after(NA // 2, NA % 2, None)
        with ExitStack() as cb:
            def sbb(name, shape, dt=F32):
                return cb.enter_context(nc.sbuf_tensor(name, shape, dt))

            hxb = sbb("hxb", [128, 2, D])
            upp = sbb("upp", [128, 2, KF, 128])
            act_a = sbb("act_a", [128, KF, 128])
            hid = sbb("hid", [128, KF, 128])
            silu2 = sbb("silu2", [128, NE // 128, 128])
            erel = sbb("erel", [128, PH, T8])
            zsum = sbb("zsum", [128, PH])
            rz = sbb("rz", [128, PH])
            pair = sbb("pair", [128, PH, XR, NK])
            epair = sbb("epair", [128, PH, XR, NK])
            picked = sbb("picked", [128, PH])
            picked_sum = sbb("picked_sum", [128, 1])
            heads_one = sbb("heads_one", [128, 1])
            neg_mean = sbb("neg_mean", [128, 1])
            shift = sbb("shift", [128, 1])
            coef = sbb("coef", [128, 2, NE])
            wT = sbb("wT", [128, NE // 128, 128])
            res = sbb("res", [128, 2, D])

            stored = [q["stored0"], q["stored1"]]
            block = cb.enter_context(nc.Block())

            def rows_at(t):
                return N - 128 if isinstance(t, int) and t == NB - 1 else t * 128

            @block.sync
            def _(sp):
                def load_h(t, j, u):
                    if late(t, 2):
                        sp.wait_ge(q["hf_ready"], t - 1)
                        sp.wait_ge(q["hxb_ready"], t - 1)
                    sp.dma_start(hx[:, u, :], h1_dram[bass.ds(rows_at(t), 128), :]).then_inc(h_loaded[u], 16)

                def store(t, j, u):
                    sp.wait_ge(q["res_ready"], t + 1)
                    new = N - (NB - 1) * 128 if isinstance(t, int) and t == NB - 1 else 128
                    sp.dma_start(out[bass.ds(rows_at(t) + 128 - new, new), :],
                                 res[128 - new:128, u, :]).then_inc(stored[u], 16)

                def body(j, u, has):
                    if has(3) and late(tile_at(j, u, 3)[0], 2):
                        load_h(*tile_at(j, u, 3))
                    if has(-1):
                        store(*tile_at(j, u, -1))

                steps(sp, body, NB, 4, 1)
                for u in (0, 1):
                    sp.wait_ge(stored[u], 16 * ((NB + 1 - u) // 2))

            @block.gpsimd
            def _(pool):
                pool.memset(heads_one[:, :], float(PH)).then_inc(q["const_ready"], 1)

                def body(j, u, has):
                    if has(1):
                        t, _, tu = tile_at(j, u, 1)
                        pool.wait_ge(h_loaded[tu], 16 * (tile_at(j, u, 1)[1] + 1))
                        if late(t, 2):
                            pool.wait_ge(q["res_ready"], t - 1)
                        pool.tensor_tensor(hxb[:, tu, :], hx[:, tu, :], bd[:, :], ALU.add).then_inc(q["hxb_ready"], 1)
                    if has(2) and late(tile_at(j, u, 2)[0], 2):
                        t, _, tu = tile_at(j, u, 2)
                        pool.wait_ge(q["mvf_ready"], t + 1)
                        pool.tensor_tensor(neg_mean[:, :], mvf[:, tu, 0:1], minus_one[:, :],
                                           ALU.mult).then_inc(q["neg_mean_ready"], 1)
                        pool.tensor_tensor(vef[:, :], mvf[:, tu, 1:2], eps[:, :], ALU.add).then_inc(q["vef_ready"], 1)
                        pool.wait_ge(q["vef_ready"], t + 1)
                        pool.tensor_tensor(rstdf[:, tu:tu + 1], vef[:, :], mhalf[:, :],
                                           ALU.pow).then_inc(q["rstdf_ready"], 1)
                        pool.wait_ge(q["neg_mean_ready"], t - 1)
                        pool.wait_ge(q["rstdf_ready"], t + 1)
                        pool.wait_ge(q["hf_ready"], t)
                        pool.tensor_tensor(shift[:, :], neg_mean[:, :], rstdf[:, tu:tu + 1],
                                           ALU.mult).then_inc(q["shift_ready"], 1)

                steps(pool, body, NB, 2, 1)

            @block.vector
            def _(dve):
                dve.wait_ge(q["const_ready"], 1)

                def stats(t, j, u):
                    dve.wait_ge(h_loaded[u], 16 * (j + 1))
                    dve.bn_stats(stf[:, u, :], hx[:, u, :]).then_inc(q["stf_ready"], 1)

                def aggregate(t, j, u):
                    if isinstance(t, int):
                        dve.wait_ge(q["stf_ready"], t + 1)
                    dve.bn_aggr(mvf[:, u, :], stf[:, u, :]).then_inc(q["mvf_ready"], 1)

                def split_hfT(t, j, u):
                    dve.wait_ge(q["hi_ready"], t + 1)
                    if late(t, 1):
                        dve.wait_ge(q["sim_ps"], t)
                    dve.tensor_tensor(hfT_lo[:, :, :], hfT[:, :, :], hfT_hi[:, :, :],
                                      ALU.subtract).then_inc(q["lo_ready"], 1)

                def expert_silu(t, j, u):
                    if late(t, 1):
                        dve.wait_ge(q["wT_ready"], t)
                    dve.wait_ge(q["e_tanh"], t + 1)
                    dve.scalar_tensor_tensor(silu2[:, :, :].rearrange("p a b -> p (a b)"),
                                             de_t[:, :, :].rearrange("p a b -> p (a b)"), 1.0,
                                             ps_e[:, :, :].rearrange("p a b -> p (a b)"),
                                             ALU.add, ALU.mult).then_inc(q["silu_ready"], 1)

                def normaliser(t, j, u):
                    dve.wait_ge(q["erel_ready"], t + 1)
                    dve.tensor_reduce(zsum[:, :], erel[:, :, :], AX, ALU.add).then_inc(q["z_ready"], 1)
                    dve.wait_ge(q["z_ready"], t + 1)
                    dve.reciprocal(rz[:, :], zsum[:, :]).then_inc(q["rz_ready"], 1)

                def pair_sums(t, j, u, n):
                    if n == 0:
                        dve.wait_ge(q["grid_ready"], t + 1)
                    dve.tensor_tensor(pair[:, n, :, :],
                                      sims[:, u, 0, n, 0:XR].unsqueeze(2).to_broadcast([128, XR, NK]),
                                      sims[:, u, 1, n, :].unsqueeze(1).to_broadcast([128, XR, NK]),
                                      ALU.add).then_inc(q["pair_ready"], 1)

                def pick(t, j, u, n):
                    dve.wait_ge(q["epair_ready"], PH * t + n + 1)
                    dve.scalar_tensor_tensor(pair[:, n, :, :].rearrange("p a b -> p (a b)"),
                                             pair[:, n, :, :].rearrange("p a b -> p (a b)"), best[:, n, T8 - 1:T8],
                                             epair[:, n, :, :].rearrange("p a b -> p (a b)"),
                                             ALU.is_ge, ALU.mult, accum_out=picked[:, n:n + 1]).then_inc(q["picked_ready"], 1)

                def add_heads(t, j, u, n):
                    dve.wait_ge(q["picked_ready"], PH * t + n + 2)
                    if n and not isinstance(t, int):
                        dve.wait_ge(q["sims_ready"], t + 2)
                    a, b, done = (n, n + 1, q["half_ready"] if n else q["coef_ready"])
                    dve.tensor_tensor(coef[:, n // 2, :], pair[:, a, :, :].rearrange("p a b -> p (a b)"),
                                      pair[:, b, :, :].rearrange("p a b -> p (a b)"), ALU.add).then_inc(done, 1)

                def rest_of(t, j, u):
                    dve.wait_ge(q["picked_ready"], PH * t + PH)
                    dve.tensor_reduce(picked_sum[:, :], picked[:, :], AX, ALU.add).then_inc(q["sum_ready"], 1)

                def add_rest(t, j, u):
                    dve.wait_ge(q["half_ready"], t + 1)
                    dve.wait_ge(q["sum_ready"], t + 1)
                    dve.scalar_tensor_tensor(coef[:, 1, NE - 1:NE], coef[:, 1, NE - 1:NE], picked_sum[:, 0:1],
                                             heads_one[:, :], ALU.subtract, ALU.add).then_inc(q["coef_ready"], 1)

                def weights(t, j, u):
                    dve.wait_ge(q["coefT_ps"], t + 1)
                    dve.wait_ge(q["silu_ready"], t + 1)
                    if late(t, 1):
                        dve.wait_ge(q["out_ps"], t)
                    dve.scalar_tensor_tensor(wT[:, :, :].rearrange("p a b -> p (a b)"),
                                             silu2[:, :, :].rearrange("p a b -> p (a b)"), 0.5,
                                             ps_g[:, :, :].rearrange("p a b -> p (a b)"),
                                             ALU.mult, ALU.mult).then_inc(q["wT_ready"], 1)

                def mlp_a(t, j, u):
                    if not isinstance(t, int):
                        dve.wait_ge(q["stf_ready"], t + 3)
                    dve.wait_ge(q["gate_t_ready"], t + 1)
                    dve.scalar_tensor_tensor(act_a[:, :, :], gate_t[:, u, :, :], 1.0, gate[:, u, :, :],
                                             ALU.add, ALU.mult).then_inc(q["act_ready"], 1)

                def mlp_b(t, j, u):
                    dve.wait_ge(q["act_ready"], t + 1)
                    dve.wait_ge(q["up_ready"], t + 1)
                    if late(t, 1):
                        dve.wait_ge(q["out_ps"], t)
                    dve.scalar_tensor_tensor(hid[:, :, :], act_a[:, :, :], 0.5, upp[:, u, :, :],
                                             ALU.mult, ALU.mult).then_inc(q["hid_ready"], 1)

                def result(t, j, u):
                    dve.wait_ge(q["hxb_ready"], t + 1)
                    dve.wait_ge(q["out_ps"], t + 1)
                    if late(t, 2):
                        dve.wait_ge(stored[u], 16 * j)
                    dve.tensor_tensor(res[:, u, :], ps_out[:, 0:D], hxb[:, u, :], ALU.add).then_inc(q["res_ready"], 1)

                def body(j, u, has):
                    now, nxt, prv = tile_at(j, u, 0), tile_at(j, u, 1), tile_at(j, u, -1)
                    second = tile_at(j, u, 2)
                    norm_second = has(2) and late(second[0], 2)
                    best_due = has(0) and late(now[0], 1)
                    if best_due:
                        top_keys(dve, *now)
                    if has(-1):
                        weights(*prv)
                    if best_due:
                        top_pairs(dve, *now)
                    if has(0):
                        pair_sums(*now, 0)
                    if has(0) and not best_due:
                        split_hfT(*nxt)
                        expert_silu(*now)
                    if best_due:
                        best_pairs(dve, *now)
                        relative(dve, *now)
                    if has(0):
                        pair_sums(*now, 1)
                    if has(1) and late(nxt[0], 2):
                        split_hfT(*nxt)
                    if has(0):
                        normaliser(*now)
                    if best_due:
                        expert_silu(*now)
                    if has(0):
                        pair_sums(*now, 2)
                        pair_sums(*now, 3)
                    if has(-1):
                        result(*prv)
                    if norm_second:
                        stats(*second)
                    if has(0):
                        mlp_a(*now)
                    if norm_second:
                        aggregate(*second)
                    if has(0):
                        pick(*now, 0)
                        mlp_b(*now)
                        pick(*now, 1)
                        pick(*now, 2)
                        add_heads(*now, 0)
                        pick(*now, 3)
                        rest_of(*now)
                        add_heads(*now, 2)
                        add_rest(*now)

                steps(dve, body, NB, 2, 1)

            @block.scalar
            def _(act):
                def copy_hfT(t, j, u):
                    act.wait_ge(q["hfT_ps"], t + 1)
                    act.activation(hfT[:, :, :], ps_m[:, 0:D].rearrange("p (k c) -> p k c", k=KD),
                                   ACT.Copy).then_inc(q["hfT_ready"], 1)
                    act.activation(hfT_hi[:, :, :], ps_m[:, 0:D].rearrange("p (k c) -> p k c", k=KD),
                                   ACT.Copy).then_inc(q["hi_ready"], 1)

                def norm(t, j, u):
                    act.wait_ge(q["shift_ready"], t - 1)
                    act.wait_ge(q["hfT_ps"], t)
                    act.activation(hf[:, :], hx[:, u, :], ACT.Identity, bias=shift[:, 0:1],
                                   scale=rstdf[:, u:u + 1]).then_inc(q["hf_ready"], 1)

                def copy_sims(t, j, u):
                    act.wait_ge(q["sim_ps"], t + 1)
                    act.activation(sims[:, u, :, :, :].rearrange("p a b c -> p (a b c)"), ps_m[:, :],
                                   ACT.Copy).then_inc(q["sims_ready"], 1)

                def ups(t, j, u):
                    act.wait_ge(q["up_ps"], t + 1)
                    for m in range(KF):
                        i = act.activation(upp[:, u, m, :], ps_u[:, m // 4, (m % 4) * 128:(m % 4 + 1) * 128],
                                           ACT.Identity, bias=bu[:, m:m + 1])
                    i.then_inc(q["up_ready"], 1)

                def exp_best(t, j, u):
                    act.wait_ge(q["rel_ready"], t + 1)
                    act.activation(erel[:, :, :], rel[:, :, :], ACT.Exp).then_inc(q["erel_ready"], 1)

                def shares(t, j, u, n):
                    act.wait_ge(q["negm_ready"], t + 1)
                    act.wait_ge(q["pair_ready"], PH * t + n + 1)
                    act.activation(epair[:, n, :, :], pair[:, n, :, :], ACT.Exp,
                                   bias=neg_m[:, n:n + 1]).then_inc(q["exp_ready"], 1)
                    act.wait_ge(q["exp_ready"], PH * t + n + 1)
                    act.wait_ge(q["rz_ready"], t + 1)
                    act.activation(epair[:, n, :, :], epair[:, n, :, :], ACT.Copy,
                                   scale=rz[:, n:n + 1]).then_inc(q["epair_ready"], 1)

                def body(j, u, has):
                    now, nxt = tile_at(j, u, 0), tile_at(j, u, 1)
                    if has(0) and late(now[0], 1):
                        exp_best(*now)
                    if has(1) and late(nxt[0], 1):
                        copy_hfT(*nxt)
                    if has(0) and not late(now[0], 1):
                        exp_best(*now)
                        ups(*now)
                    if has(0):
                        shares(*now, 0)
                        shares(*now, 1)
                    if has(1) and late(nxt[0], 1):
                        copy_sims(*nxt)
                    if has(0):
                        shares(*now, 2)
                    if has(1) and late(nxt[0], 1):
                        expert_tanh(act, *nxt)
                    if has(0):
                        shares(*now, 3)
                    if has(1) and late(nxt[0], 1):
                        gates(act, *nxt)
                    if has(2) and late(tile_at(j, u, 2)[0], 2):
                        norm(*tile_at(j, u, 2))
                    if has(1) and late(nxt[0], 1):
                        ups(*nxt)

                steps(act, body, NB, 2, 1)

            @block.tensor
            def _(pe):
                def transpose_h(t, j, u):
                    pe.wait_ge(q["hf_ready"], t + 1)
                    if late(t, 1):
                        pe.wait_ge(q["sims_ready"], t)
                    for k in range(KD):
                        i = pe.transpose(ps_m[:, k * 128:(k + 1) * 128], hf[:, k * 128:(k + 1) * 128], ident[:, :])
                    i.then_inc(q["hfT_ps"], 1)

                def similarities(t, j, u):
                    pe.wait_ge(q["hfT_ready"], t + 1)
                    pe.wait_ge(q["lo_ready"], t + 1)
                    sim_products(pe).then_inc(q["sim_ps"], 1)

                def experts(t, j, u):
                    pe.wait_ge(q["silu_ready"], t)
                    by_feature(pe, ps_e, down, range(KF)).then_inc(q["e_ps"], 1)

                def gate_up(t, j, u):
                    if late(t, 2):
                        pe.wait_ge(q["wT_ready"], t - 1)
                    else:
                        pe.wait_ge(q["gate_ready"], t)
                    by_feature(pe, ps_g, wg, range(KF)).then_inc(q["gate_ps"], 1)
                    pe.wait_ge(q["up_ready"], t)
                    by_feature(pe, ps_u, wu, range(KF)).then_inc(q["up_ps"], 1)

                def mlp_out(t, j, u):
                    pe.wait_ge(q["hid_ready"], t + 1)
                    if late(t, 1):
                        pe.wait_ge(q["res_ready"], t)
                    for m in range(KF):
                        pe.matmul(ps_out[:, 0:D], hid[:, m, :], wd[:, m, :], start=m == 0, stop=False)

                def transpose_coef(t, j, u, has_next):
                    if has_next:
                        pe.wait_ge(q["gate_ready"], t + 2)
                    for half in range(2):
                        pe.wait_ge(q["coef_ready"], 2 * t + half + 1)
                        for m in range(NE // 128):
                            i = pe.matmul(ps_g[:, m // 4, (m % 4) * 128:(m % 4 + 1) * 128],
                                          coef[:, half, m * 128:(m + 1) * 128], ident[:, :],
                                          start=half == 0 and m % 4 == 0, stop=half == 1 and m % 4 == 3,
                                          is_transpose=True)
                    i.then_inc(q["coefT_ps"], 1)

                def experts_out(t, j, u):
                    pe.wait_ge(q["wT_ready"], t + 1)
                    for m in range(NE // 128):
                        i = pe.matmul(ps_out[:, 0:D], wT[:, m, :], up[:, m, :], start=False, stop=m == NE // 128 - 1)
                    i.then_inc(q["out_ps"], 1)

                def body(j, u, has):
                    now, nxt, prv = tile_at(j, u, 0), tile_at(j, u, 1), tile_at(j, u, -1)
                    if has(-1) and has(0):
                        mlp_out(*prv)
                    front = has(1) and late(nxt[0], 1)
                    if front:
                        transpose_h(*nxt)
                    if has(-1):
                        experts_out(*prv)
                    if front:
                        similarities(*nxt)
                        experts(*nxt)
                        gate_up(*nxt)
                    if has(0) and not has(1):
                        mlp_out(*now)
                    if has(0):
                        transpose_coef(*now, has(1))

                steps(pe, body, NB, 2, 1)


def kernel(**inputs):
    import numpy as np
    import concourse.bacc as bacc
    from concourse.bass_utils import run_bass_kernel_spmd

    a = {k.replace("L0_", ""): np.asarray(v) for k, v in inputs.items()}

    def rows(w):
        return np.ascontiguousarray(w.reshape(-1, 128, w.shape[1]).transpose(1, 0, 2))

    def cols(b):
        return np.ascontiguousarray(b.reshape(-1, 128).T)

    n = IMG // P
    patches = a["x"].reshape(B, CH, n, P, n, P).transpose(0, 2, 4, 3, 5, 1).reshape(B, NP_, PD)
    x = np.zeros((NA, C, PD), np.float32)
    for t in range(NA):
        for g in range(G):
            x[t, g * S + 1:(g + 1) * S] = patches[min(G * t, B - G) + g]

    image = np.zeros((G, C), np.float32)
    for g in range(G):
        image[g, g * S:(g + 1) * S] = 1.0
    image_q = image.copy()
    image_q[0, R] = 1.0
    ones = np.ones((1, C), np.float32)
    far, near_k, near_q = -BIG * ones, BIG * image, BIG * image_q
    mask = np.concatenate([
        np.concatenate([ones, image_q]), np.concatenate([ones, image]),
        np.tile(np.concatenate([far, near_k]), (1, HB)), np.tile(np.concatenate([far, near_q]), (1, HB)),
    ], axis=1)
    feeds = {
        "x": x,
        "ident": np.eye(128, dtype=np.float32),
        "nident": -np.eye(C, dtype=np.float32),
        "headmask": np.kron(np.eye(HC, dtype=np.float32), np.ones((DK, 1), np.float32)),
        "mask": mask,
        "ln1_w": cols(a["tok_ln1_w"]), "ln1_b": cols(a["tok_ln1_b"]),
        "lin_w": rows(a["tok_lin_w"]), "lin_b": a["tok_lin_b"][None],
        "ln2_w": a["tok_ln2_w"][None], "ln2_b": a["tok_ln2_b"][None],
        "cls": a["tok_cls_token"][0], "pos": a["tok_pos_embedding"][0],
        "wq": rows(a["attn_Wq"].T), "wk": rows(a["attn_Wk"].T), "wv": rows(a["attn_Wv"].T),
        "wo": rows(a["attn_Wo"].T),
        "bq": cols(a["attn_bq"]), "bk": cols(a["attn_bk"]),
        "bv": a["attn_bv"][None], "bo": a["attn_bo"][None],
        "wg": rows(a["ffn_Wg"]), "wu": rows(a["ffn_Wu"]), "wd": rows(a["ffn_Wd"]),
        "bg": cols(a["ffn_bg"]), "bu": cols(a["ffn_bu"]), "bd": a["ffn_bd"][None],
        "wqf": np.ascontiguousarray(a["ffn_Wq"].reshape(D, 2 * PH, RET).transpose(2, 1, 0)),
        "keys": np.ascontiguousarray(a["ffn_keys"].transpose(3, 2, 0, 1).reshape(RET, 2 * PH, NK)),
        "down": rows(a["ffn_down_embed"].T), "up": rows(a["ffn_up_embed"]),
    }
    feeds = {f"in_{k}": np.ascontiguousarray(v) for k, v in feeds.items()}
    nc = bacc.Bacc("TRN2", target_bir_lowering=False, num_devices=1)
    args = {k[3:]: nc.dram_tensor(k, v.shape, F32, kind="ExternalInput").ap() for k, v in feeds.items()}
    out = nc.dram_tensor("out", (N, D), F32, kind="ExternalOutput").ap()
    h1_dram = nc.dram_tensor("h1_dram", (N, D), F32, kind="Internal").ap()
    vit_tower(nc, args, out, h1_dram)
    r = run_bass_kernel_spmd(nc, [feeds], core_ids=[0])
    return r.results[0]["out"].reshape(B, S, D)
```
